# Optimizing a Trainium2 kernel written in Bass

```python
import numpy as np
import jax
import jax.numpy as jnp

def _softmax(x, axis=-1):
    return jax.nn.softmax(x, axis=axis)
def _gelu(x):
    return jax.nn.gelu(x, approximate=True)
def _silu(x):
    return jax.nn.silu(x)
def _sigmoid(x):
    return jax.nn.sigmoid(x)
def _layernorm(x, axis=-1, eps=1e-5):
    m = jnp.mean(x, axis=axis, keepdims=True)
    v = jnp.var(x, axis=axis, keepdims=True)
    return (x - m) / jnp.sqrt(v + eps)
def _scatter_add(tgt, idx, src, axis=0):
    return tgt.at[idx].add(src)
def _segment_sum(src, seg, n):
    return jax.ops.segment_sum(src, seg, n)

kernel_name = 'mk_conv_seq_d1_conv_nchw64_848e58'

def setup_inputs(seed: int = 0):
    np.random.seed(seed)
    _w = jnp.asarray
    def _rec_inputs():
        import jax
        import jax.numpy as jnp
        _gk = jax.random.key(seed)
        x = -0.000125 + 0.9999 * jax.random.normal(jax.random.fold_in(_gk, 1), (8, 64, 256, 256), jnp.float32)
        return x
    x = _rec_inputs()
    def _L0_conv_setup():
        import jax, jax.numpy as jnp
        import numpy as np
        from jax import lax
        P = 8
        DN = ('NCHW', 'OIHW', 'NCHW')
        key = jax.random.key(seed)
        ks = jax.random.split(key, 8)
        B, D, H, W = (8, 64, 256, 256)
        C = 4 * D
        return {'x': jax.random.normal(ks[0], (B, D, H, W), jnp.float32), 'w_in': jax.random.normal(ks[1], (C, D, 1, 1), jnp.float32) * 0.05, 'b_in': jax.random.normal(ks[2], (C,), jnp.float32) * 0.05, 'fft_filter': jnp.ones((C, 1, 1, P, P // 2 + 1), jnp.float32), 'w_dw': jax.random.normal(ks[3], (C, 1, 7, 7), jnp.float32) * 0.05, 'b_dw': jax.random.normal(ks[4], (C,), jnp.float32) * 0.05, 'w_out': jax.random.normal(ks[5], (D, C, 1, 1), jnp.float32) * 0.05, 'b_out': jax.random.normal(ks[6], (D,), jnp.float32) * 0.05}
    _L0_conv_all = _L0_conv_setup()
    _L0_conv_in = {k: v for k, v in _L0_conv_all.items() if k in ('w_in', 'b_in', 'fft_filter', 'w_dw', 'b_dw', 'w_out', 'b_out', )}
    del _L0_conv_all

    return {
        "x": x,
        "L0_conv_w_in": _L0_conv_in["w_in"],
        "L0_conv_b_in": _L0_conv_in["b_in"],
        "L0_conv_fft_filter": _L0_conv_in["fft_filter"],
        "L0_conv_w_dw": _L0_conv_in["w_dw"],
        "L0_conv_b_dw": _L0_conv_in["b_dw"],
        "L0_conv_w_out": _L0_conv_in["w_out"],
        "L0_conv_b_out": _L0_conv_in["b_out"],
    }

def reference(x, L0_conv_w_in, L0_conv_b_in, L0_conv_fft_filter, L0_conv_w_dw, L0_conv_b_dw, L0_conv_w_out, L0_conv_b_out):
    import jax
    import jax.numpy as jnp
    def _L0_conv_ref(x, w_in, b_in, fft_filter, w_dw, b_dw, w_out, b_out):
        import jax, jax.numpy as jnp
        import numpy as np
        from jax import lax
        P = 8
        DN = ('NCHW', 'OIHW', 'NCHW')
        B, D, H, W = x.shape
        C = w_in.shape[0]
        x = lax.conv_general_dilated(x, w_in, (1, 1), 'SAME', dimension_numbers=DN)
        x = x + b_in[None, :, None, None]
        xp = x.reshape(B, C, H // P, P, W // P, P).transpose(0, 1, 2, 4, 3, 5)
        xf = jnp.fft.rfft2(xp)
        xf = xf * fft_filter
        xp = jnp.fft.irfft2(xf, s=(P, P))
        x = xp.transpose(0, 1, 2, 4, 3, 5).reshape(B, C, H, W)
        x = lax.conv_general_dilated(x, w_dw, (1, 1), 'SAME', dimension_numbers=DN, feature_group_count=C)
        x = x + b_dw[None, :, None, None]
        x = jax.nn.gelu(x, approximate=False)
        x = lax.conv_general_dilated(x, w_out, (1, 1), 'SAME', dimension_numbers=DN)
        return x + b_out[None, :, None, None]

    def _gn(v, G=32, eps=1e-5):
        B_, C_, H_, W_ = v.shape
        g = v.reshape(B_, G, C_ // G, H_, W_)
        m = jnp.mean(g, axis=(2, 3, 4), keepdims=True)
        s = jnp.var(g, axis=(2, 3, 4), keepdims=True)
        return ((g - m) / jnp.sqrt(s + eps)).reshape(v.shape)

    def _ln_c(v, eps=1e-6):
        m = jnp.mean(v, axis=1, keepdims=True)
        s = jnp.var(v, axis=1, keepdims=True)
        return (v - m) / jnp.sqrt(s + eps)

    def _ln_t(v, eps=1e-5):
        m = jnp.mean(v, axis=-1, keepdims=True)
        s = jnp.var(v, axis=-1, keepdims=True)
        return (v - m) / jnp.sqrt(s + eps)

    def _to_tokens(v):
        B_, C_, H_, W_ = v.shape
        return v.reshape(B_, C_, H_ * W_).transpose(0, 2, 1)
    def _from_tokens(t, like):
        B_, C_, H_, W_ = like.shape
        return t.transpose(0, 2, 1).reshape(B_, C_, H_, W_)

    x = _L0_conv_ref(x, L0_conv_w_in, L0_conv_b_in, L0_conv_fft_filter, L0_conv_w_dw, L0_conv_b_dw, L0_conv_w_out, L0_conv_b_out)
    return x


_drawn_inputs = setup_inputs


def setup_inputs(seed=0):
    import zlib

    import numpy as np

    out = dict(_drawn_inputs(seed))
    spreads = {'L0_conv_fft_filter': (1.0, 0.2)}
    factors = {}
    for name, (base, spread) in spreads.items():
        noise = np.random.default_rng([zlib.crc32(name.encode()), seed]).standard_normal(out[name].shape)
        drawn = base * np.exp(spread * noise) if base else spread * noise
        out[name] = jnp.asarray(drawn.astype(out[name].dtype))
    for name, factor in factors.items():
        out[name] = (out[name] * factor).astype(out[name].dtype)
    return out
```

```python
from contextlib import ExitStack

import numpy as np

import concourse.bass as bass
from concourse import mybir
from concourse.alu_op_type import AluOpType as ALU

F32 = mybir.dt.float32
F32R = mybir.dt.float32r
ACT = mybir.ActivationFunctionType

PATCH = 8
TAPS = 7
HALO = TAPS // 2
SPREAD = PATCH + 2 * HALO
BLK_Y, BLK_X = 2 * PATCH, PATCH
PX = BLK_Y * BLK_X
REACH_Y, REACH_X = 2 * BLK_Y, 2 * BLK_X
REACH = REACH_Y * REACH_X
GRP = 4
IMG = 2
BANK = 512


def real(ap):
    return ap.bitcast(F32R)


class Named:

    def __init__(self, nc, ctx, stage):
        self.nc, self.ctx, self.stage = nc, ctx, stage

    def sbuf(self, name, shape):
        return self.ctx.enter_context(self.nc.sbuf_tensor(f"{self.stage}_{name}", shape, F32))

    def psum(self, name, shape):
        return self.ctx.enter_context(self.nc.psum_tensor(f"{self.stage}_{name}", shape, F32))

    def sem(self, name):
        return self.ctx.enter_context(self.nc.semaphore(f"{self.stage}_{name}"))


def build_composites(nc, filt_t, wdw_t, circ_c, shift_c, e_dram):
    freqs, C = filt_t.shape
    taps = wdw_t.shape[0]
    PP = PATCH * PATCH
    SS = SPREAD * SPREAD
    CQ = C // 4
    K_MM = 4 * BANK // C
    D_MM = 4 * BANK // CQ
    K_GROUPS = PP // K_MM
    D_GROUPS = -(-SS // D_MM)
    UNITS = CQ // GRP
    with ExitStack() as ctx:
        n = Named(nc, ctx, "comp")
        filt = n.sbuf("filt", [freqs, C])
        wdw = n.sbuf("wdw", [taps, C])
        circ_tab = n.sbuf("circ_tab", [freqs, PATCH, 2 * PATCH, PATCH])
        shift_tab = n.sbuf("shift_tab", [taps, SPREAD, 3 * TAPS, PATCH])
        circ = n.sbuf("circ", [PP, PP, C])
        shifted = n.sbuf("shifted", [PP, SS, CQ])
        lhs = n.sbuf("lhs", [PP, 2, GRP, 2, PP])
        stage = n.sbuf("stage", [128, 2, GRP, REACH_Y, REACH_X])
        ps = [n.psum(f"ps{i}", [128, 4, BANK]) for i in range(2)]
        loaded = n.sem("loaded")
        zeroed = n.sem("zeroed")
        mm_done = n.sem("mm_done")
        ev_act = n.sem("ev_act")
        ev_dve = n.sem("ev_dve")
        lhs_ready = n.sem("lhs_ready")
        comp_done = n.sem("comp_done")
        top_done = n.sem("top_done")
        bot_done = n.sem("bot_done")
        stored = [n.sem(f"stored{i}") for i in range(2)]
        block = ctx.enter_context(nc.Block())

        table0 = [K_GROUPS + q * D_GROUPS for q in range(4)]

        def groups_by(parity, upto):
            return (upto + 1 - parity) // 2

        def evacuate(eng, t, parity, copy):
            eng.wait_ge(mm_done, t + 1)
            if t < K_GROUPS:
                copy(circ[:, t * K_MM:(t + 1) * K_MM, :].rearrange("p a c -> p (a c)"),
                     ps[t % 2][0:PP, :, :].rearrange("p a c -> p (a c)")).then_inc((ev_dve, ev_act)[parity], 1)
            else:
                g = (t - K_GROUPS) % D_GROUPS
                cnt = min(D_MM, SS - g * D_MM)
                copy(shifted[:, g * D_MM:g * D_MM + cnt, :].rearrange("p a c -> p (a c)"),
                     ps[t % 2][0:PP, :, :].rearrange("p a c -> p (a c)")[:, 0:cnt * CQ]
                     ).then_inc((ev_dve, ev_act)[parity], 1)

        @block.sync
        def _(sp):
            sp.dma_start(filt[:], filt_t).then_inc(loaded, 16)
            sp.dma_start(wdw[:], wdw_t).then_inc(loaded, 16)
            sp.dma_start(circ_tab[:], circ_c).then_inc(loaded, 16)
            sp.dma_start(shift_tab[:], shift_c).then_inc(loaded, 16)
            for q in range(4):
                with sp.Fori(0, UNITS // 2) as i:
                    for k in range(2):
                        u = i * 2 + (q * UNITS + k)
                        sp.wait_ge(top_done, u * 2 + 2)
                        sp.wait_ge(bot_done, u * 2 + 2)
                        sp.dma_start(e_dram[u, :, :, :], stage[:, k].rearrange("p c r x -> p c (r x)")
                                     ).then_inc(stored[k], 16)
            for k in range(2):
                sp.wait_ge(stored[k], 16 * 2 * UNITS)

        @block.tensor
        def _(pe):
            pe.wait_ge(loaded, 64)

            def free(t):
                if t >= 2:
                    pe.wait_ge((ev_dve, ev_act)[t % 2], groups_by(t % 2, t - 1))

            for t in range(K_GROUPS):
                free(t)
                for m in range(K_MM):
                    y, x = divmod(t * K_MM + m, PATCH)
                    at = m * C
                    mm = pe.matmul(ps[t % 2][0:PP, at // BANK, at % BANK:at % BANK + C],
                                   circ_tab[:, x, PATCH - y:2 * PATCH - y, :].rearrange("p u v -> p (u v)"), filt[:, :],
                                   start=True, stop=True)
                mm.then_inc(mm_done, 1)
            for q in range(4):
                if q:
                    pe.wait_ge(comp_done, q * UNITS)
                    pe.wait_ge(top_done, 2 * q * UNITS)
                    pe.wait_ge(bot_done, 2 * q * UNITS)
                for g in range(D_GROUPS):
                    t = table0[q] + g
                    free(t)
                    for m in range(min(D_MM, SS - g * D_MM)):
                        Y, X = divmod(g * D_MM + m, SPREAD)
                        at = m * CQ
                        mm = pe.matmul(ps[t % 2][0:PP, at // BANK, at % BANK:at % BANK + CQ],
                                       shift_tab[:, X, SPREAD - 1 - Y:SPREAD - 1 - Y + PATCH, :]
                                       .rearrange("p u v -> p (u v)"),
                                       wdw[:, q * CQ:(q + 1) * CQ], start=True, stop=True)
                    mm.then_inc(mm_done, 1)
                pe.wait_ge(ev_dve, groups_by(0, table0[q] + D_GROUPS))
                pe.wait_ge(ev_act, groups_by(1, table0[q] + D_GROUPS))
                with pe.Fori(0, UNITS // 2) as i:
                    for k in range(2):
                        u = i * 2 + (q * UNITS + k)
                        pe.wait_ge(lhs_ready, u * 2 + 2)
                        if k == 1:
                            pe.wait_ge(top_done, u * 2 - 2)
                            pe.wait_ge(bot_done, u * 2 - 2)
                        else:
                            pe.wait_ge(top_done, u * 2)
                            pe.wait_ge(bot_done, u * 2)
                        for j in range(GRP):
                            mm = pe.matmul(ps[k][:, j // 2, (j % 2) * SS:(j % 2 + 1) * SS],
                                           lhs[:, k, j].rearrange("p h a -> p (h a)"),
                                           shifted[:, :, bass.ds(i * (2 * GRP) + (k * GRP + j), 1)]
                                           .rearrange("p a c -> p (a c)"),
                                           start=True, stop=True)
                        mm.then_inc(comp_done, 1)

        def composites(eng, q, part, done, copy, before):
            rows = slice(0, PP) if part == 0 else slice(PP, 128)
            r0 = PATCH * part
            with eng.Fori(0, UNITS // 2) as i:
                for k in range(2):
                    u = i * 2 + (q * UNITS + k)
                    before(i, k, u)
                    eng.wait_ge(comp_done, u + 1)
                    eng.wait_ge(stored[k], i * 16 + q * UNITS // 2 * 16)
                    for b in range(GRP // 2):
                        copy(stage[rows, k, 2 * b:2 * b + 2, r0:r0 + SPREAD, 0:SPREAD],
                             ps[k][rows, b, 0:2 * SS].rearrange("p (c r x) -> p c r x", c=2, x=SPREAD)
                             ).then_inc(done, 1)

        @block.scalar
        def _(act):
            act.wait_ge(zeroed, 1)
            for t in range(1, K_GROUPS, 2):
                evacuate(act, t, 1, act.copy)
            for q in range(4):
                for t in range(table0[q], table0[q] + D_GROUPS):
                    if t % 2 == 1:
                        evacuate(act, t, 1, act.copy)
                composites(act, q, 0, top_done, act.copy, lambda i, k, u: None)

        @block.vector
        def _(dve):
            dve.memset(stage[:], 0.0).then_inc(zeroed, 1)
            dve.wait_ge(zeroed, 1)
            for t in range(0, K_GROUPS, 2):
                evacuate(dve, t, 0, dve.tensor_copy)
            for q in range(4):
                for t in range(table0[q], table0[q] + D_GROUPS):
                    if t % 2 == 0:
                        evacuate(dve, t, 0, dve.tensor_copy)
                dve.wait_ge(ev_dve, groups_by(0, K_GROUPS))
                dve.wait_ge(ev_act, groups_by(1, K_GROUPS))

                def pick(i, k, u):
                    if k == 1:
                        dve.wait_ge(comp_done, u - 1)
                    else:
                        dve.wait_ge(comp_done, u)
                    for half in range(2):
                        dve.tensor_copy(lhs[:, k, :, half, :],
                                        circ[:, :, bass.ds(i * (2 * GRP) + (q * CQ + k * GRP), GRP)]
                                        .rearrange("p a c -> p c a")).then_inc(lhs_ready, 1)

                composites(dve, q, 1, bot_done, dve.tensor_copy, pick)


def conv_in(nc, x, w_in_t, h_dram):
    B, D, H, W = x.shape
    C = w_in_t.shape[1]
    PAIRS, BY, BX = B // IMG, H // BLK_Y, W // BLK_X
    HW, HX = W // 2, BX // 2
    STRIPS = PAIRS * BY
    BLKS = HX * IMG
    SETS = 2 * C * BLKS // (8 * BANK)
    PER = BLKS // SETS
    with ExitStack() as ctx:
        n = Named(nc, ctx, "cin")
        xs = n.sbuf("xs", [128, 2, IMG, BLK_Y, W])
        xsplit = n.sbuf("xsplit", [128, 2, IMG, HX, PX])
        hs = n.sbuf("hs", [128, 2, C, BLKS])
        w = n.sbuf("w", [128, C])
        whi = n.sbuf("whi", [128, C])
        wlo = n.sbuf("wlo", [128, C])
        ps = [n.psum(f"ps{i}", [128, 4, BANK]) for i in range(2)]
        w_loaded = n.sem("w_loaded")
        w_split = n.sem("w_split")
        x_loaded = [n.sem(f"x_loaded{i}") for i in range(2)]
        x_hi = n.sem("x_hi")
        x_round = n.sem("x_round")
        x_lo = n.sem("x_lo")
        mm_done = n.sem("mm_done")
        ev_act = n.sem("ev_act")
        ev_dve = n.sem("ev_dve")
        stored = [n.sem(f"stored{i}") for i in range(2)]
        block = ctx.enter_context(nc.Block())

        h_view = [h.rearrange("g p y f j b -> y f p g (j b)") for h in h_dram]

        @block.sync
        def _(sp):
            for half in range(2):
                sp.dma_start(w[64 * half:64 * half + D, :], w_in_t).then_inc(w_loaded, 16)

            def load(q, by, k, s):
                if s is not None:
                    sp.wait_ge(x_hi, s * (2 * IMG) - 2 * IMG)
                    sp.wait_ge(x_lo, s * (2 * IMG) - 2 * IMG)
                src = x[bass.ds(q * IMG, IMG), :, bass.ds(by * BLK_Y, BLK_Y), :].rearrange("i c r w -> c i (r w)")
                for half in range(2):
                    sp.dma_start(xs[64 * half:64 * half + D, k].rearrange("p i r w -> p i (r w)"), src
                                 ).then_inc(x_loaded[k], 16)

            def store(q, by, s, f):
                sp.wait_ge(ev_act, s * SETS + SETS // 2 * (f + 1))
                sp.wait_ge(ev_dve, s * SETS + SETS // 2 * (f + 1))
                for c0 in range(0, C, C // 2):
                    sp.dma_start(h_view[q][by, f, :, c0 // GRP:(c0 + C // 2) // GRP, :],
                                 hs[:, f, c0:c0 + C // 2, :].rearrange("p (g j) b -> p g (j b)", j=GRP)
                                 ).then_inc(stored[f], 16)

            load(0, 0, 0, None)
            for q in range(PAIRS):
                with sp.Fori(0, BY // 2 - 1) as i:
                    for k in range(2):
                        s = i * 2 + (q * BY + k)
                        load(q, i * 2 + (k + 1), 1 - k, s + 1)
                        for f in range(2):
                            store(q, i * 2 + k, s, f)
                for k in range(2):
                    by = BY - 2 + k
                    s = q * BY + by
                    if s + 1 < STRIPS:
                        load((s + 1) // BY, (s + 1) % BY, 1 - k, s + 1)
                    for f in range(2):
                        store(q, by, s, f)
            for f in range(2):
                sp.wait_ge(stored[f], 16 * 2 * STRIPS)

        @block.tensor
        def _(pe):
            pe.wait_ge(w_split, 2)
            with pe.Fori(0, STRIPS) as s:
                for f in range(2):
                    pe.wait_ge(x_hi, s * (2 * IMG) + (f + 1) * IMG)
                    pe.wait_ge(x_lo, s * (2 * IMG) + (f + 1) * IMG)
                    for t in range(SETS):
                        sem = (ev_act, ev_dve)[t % 2]
                        pe.wait_ge(sem, s * SETS + f * (SETS // 2) + t // 2)
                        for m in range(PER):
                            bx, img = divmod(t * PER + m, IMG)
                            out = ps[t % 2][:, m // 2, (m % 2) * C:(m % 2 + 1) * C]
                            lhs = real(xsplit[:, f, img, bx, :])
                            pe.matmul(out, lhs, real(whi[:, :]), start=True, stop=False)
                            mm = pe.matmul(out, lhs, real(wlo[:, :]), start=False, stop=True)
                        mm.then_inc(mm_done, 1)

        def split(eng, i, m, half):
            k, f = m // 2 % 2, m % 2
            eng.wait_ge(x_loaded[k], i * 32 + 32 * (m // 4 + 1))
            if m:
                eng.wait_ge(mm_done, i * (4 * SETS) + (m - 1) * SETS)
            for img in range(IMG):
                half(i * 8 + 2 * m + img, xs[:, k, img, :, f * HW:(f + 1) * HW].rearrange("p r (b x) -> p r b x", x=BLK_X),
                     xsplit[:, f, img].rearrange("p b (r x) -> p r b x", x=BLK_X))

        def evacuate(eng, s, f, parity, copy, done):
            eng.wait_ge(stored[f], s * 32)
            for t in range(parity, SETS, 2):
                eng.wait_ge(mm_done, s * (2 * SETS) + (f * SETS + t + 1))
                copy(hs[:, f, :, t * PER:(t + 1) * PER],
                     ps[parity][:, :, :].rearrange("p a (i c) -> p c (a i)", i=2)).then_inc(done, 1)

        @block.scalar
        def _(act):
            def body(i, last):
                for m in range(4):
                    if not (last and m == 3):
                        split(act, i, m + 1, act_half)
                    evacuate(act, i * 2 + m // 2, m % 2, 0, act.copy, ev_act)

            def act_half(n_before, xin, xout):
                act.copy(real(xout[0:64]), xin[0:64]).then_inc(x_hi, 1)

            split(act, 0, 0, act_half)
            with act.Fori(0, STRIPS // 2 - 1) as i:
                body(i, False)
            body(STRIPS // 2 - 1, True)

        @block.vector
        def _(dve):
            dve.wait_ge(w_loaded, 32)
            dve.tensor_copy(real(whi[:, :]), w[:, :]).then_inc(w_split, 1)
            dve.wait_ge(w_split, 1)
            dve.tensor_tensor(real(wlo[:, :]), w[:, :], whi[:, :], ALU.subtract).then_inc(w_split, 1)

            def body(i, last):
                for m in range(4):
                    if not (last and m == 3):
                        split(dve, i, m + 1, dve_half)
                    evacuate(dve, i * 2 + m // 2, m % 2, 1, dve.tensor_copy, ev_dve)

            def dve_half(n_before, xin, xout):
                dve.tensor_copy(real(xout[64:128]), xin[64:128]).then_inc(x_round, 1)
                dve.wait_ge(x_round, n_before + 1)
                dve.tensor_tensor(real(xout[64:128]), xin[64:128], xout[64:128], ALU.subtract).then_inc(x_lo, 1)

            split(dve, 0, 0, dve_half)
            with dve.Fori(0, STRIPS // 2 - 1) as i:
                body(i, False)
            body(STRIPS // 2 - 1, True)


def spatial(nc, b_in_r, b_dw_r, e_dram, h_dram, g_dram):
    PAIRS = len(h_dram)
    GROUPS, _, BY, _, _, HALF = h_dram[0].shape
    C = GROUPS * GRP
    ROW = 2 * HALF
    N = BY * ROW
    TY, TROW = BY + 1, ROW + IMG
    CUTS = [0, 6, 12, TY]
    BANKS = len(CUTS) - 1
    UNITS = GROUPS * PAIRS
    assert PAIRS % 2 == 0 and max(b - a for a, b in zip(CUTS, CUTS[1:])) * TROW <= BANK
    with ExitStack() as ctx:
        n = Named(nc, ctx, "sp")
        b_in = n.sbuf("b_in", [128, C])
        b_dw = n.sbuf("b_dw", [128, C])
        eraw = n.sbuf("eraw", [128, GRP, REACH_Y, 2, BLK_X])
        ehi = n.sbuf("ehi", [128, GRP, 2, REACH_Y, BLK_X])
        elo = n.sbuf("elo", [128, GRP, 2, REACH_Y, BLK_X])
        h = n.sbuf("h", [128, 2, BY, 2, GRP, HALF])
        hi = n.sbuf("hi", [128, 2, BY, 2, GRP, HALF])
        g = n.sbuf("g", [128, 2, GRP, TY * TROW])
        ps = [n.psum(f"ps{i}", [128, BANKS, BANK]) for i in range(2)]
        bias = n.sbuf("bias", [128, GRP])
        b_loaded = n.sem("b_loaded")
        bias_here = n.sem("bias_here")
        e_loaded = n.sem("e_loaded")
        h_loaded = [n.sem(f"h_loaded{i}") for i in range(2)]
        e_hi = n.sem("e_hi")
        e_lo = n.sem("e_lo")
        h_hi = n.sem("h_hi")
        h_lo = n.sem("h_lo")
        mm_done = n.sem("mm_done")
        g_done = n.sem("g_done")
        stored = [n.sem(f"stored{i}") for i in range(2)]
        block = ctx.enter_context(nc.Block())

        @block.sync
        def _(sp):
            sp.dma_start(b_in[:], b_in_r.to_broadcast([128, C])).then_inc(b_loaded, 16)
            sp.dma_start(b_dw[:], b_dw_r.to_broadcast([128, C])).then_inc(b_loaded, 16)

            def load_e(c, first):
                if not first:
                    sp.wait_ge(e_lo, c * GRP)
                sp.dma_start(eraw[:].rearrange("p c r d x -> p c (r d x)"), e_dram[c, :, :, :]).then_inc(e_loaded, 16)

            def load_h(c, q, first):
                k = q % 2
                if not first:
                    sp.wait_ge(mm_done, (c * PAIRS + (q - 1)) * (GRP * BANKS))
                sp.dma_start(h[:, k].rearrange("p y f j b -> p (y f j b)"),
                             h_dram[q][c].rearrange("p y f j b -> p (y f j b)")).then_inc(h_loaded[k], 16)

            def store(c, q):
                sp.wait_ge(g_done, (c * PAIRS + (q + 1)) * (GRP * BANKS))
                sp.dma_start(g_dram[q][bass.ds(c * GRP, GRP)].rearrange("j p t -> p j t"), g[:, q % 2]
                             ).then_inc(stored[q % 2], 16)

            def step(c, last):
                for q in range(PAIRS):
                    if q + 1 < PAIRS:
                        load_h(c, q + 1, False)
                    elif not last:
                        load_e(c + 1, False)
                        load_h(c + 1, 0, False)
                    store(c, q)

            load_e(0, True)
            load_h(0, 0, True)
            with sp.Fori(0, GROUPS - 1) as c:
                step(c, False)
            step(GROUPS - 1, True)
            for k in range(2):
                sp.wait_ge(stored[k], 16 * (UNITS // 2))

        @block.vector
        def _(dve):
            dve.wait_ge(b_loaded, 32)
            with dve.Fori(0, GROUPS) as c:
                for q in range(PAIRS):
                    k = q % 2
                    dve.wait_ge(h_loaded[k], (c * (PAIRS // 2) + (q // 2 + 1)) * 16)
                    for j in range(GRP):
                        raw = h[:, k, :, :, j, :].rearrange("p y f b -> p (y f) b")
                        big = hi[:, k, :, :, j, :].rearrange("p y f b -> p (y f) b")
                        bias = b_in[:, bass.ds(c * GRP + j, 1)]
                        dve.tensor_scalar(real(big), raw, bias, None, ALU.add).then_inc(h_hi, 1)
                        dve.wait_ge(h_hi, c * (PAIRS * GRP) + (q * GRP + j + 1))
                        dve.scalar_tensor_tensor(real(raw), raw, bias, big, ALU.add, ALU.subtract
                                                 ).then_inc(h_lo, 1)
                    if q == 0:
                        dve.wait_ge(e_loaded, c * 16 + 16)
                        for j in range(GRP):
                            if True:
                                dve.wait_ge(mm_done, c * (PAIRS * GRP * BANKS))
                            raw = eraw[:, j].rearrange("p r d x -> p d r x")
                            dve.tensor_copy(real(ehi[:, j]), raw).then_inc(e_hi, 1)
                            dve.wait_ge(e_hi, c * GRP + (j + 1))
                            dve.tensor_tensor(real(elo[:, j]), raw, ehi[:, j], ALU.subtract).then_inc(e_lo, 1)

        @block.tensor
        def _(pe):
            with pe.Fori(0, GROUPS) as c:
                for q in range(PAIRS):
                    k = q % 2
                    for j in range(GRP):
                        u = q * GRP + j
                        pe.wait_ge(h_lo, c * (PAIRS * GRP) + (u + 1))
                        if q == 0:
                            pe.wait_ge(e_lo, c * GRP + (j + 1))
                        for b in range(BANKS):
                            if u < 2:
                                pe.wait_ge(g_done, c * (PAIRS * GRP * BANKS) + (u * BANKS + b + 1 - 2 * BANKS)
                                           if False else c * (PAIRS * GRP * BANKS))
                            else:
                                pe.wait_ge(g_done, c * (PAIRS * GRP * BANKS) + (u - 2) * BANKS + (b + 1))
                            t0, t1 = CUTS[b], CUTS[b + 1]
                            parts = [(dy, dx, e, v) for dy in range(2) for dx in range(2)
                                     for e, v in ((ehi, hi), (ehi, h), (elo, hi))]
                            for m, (dy, dx, e, v) in enumerate(parts):
                                r0, r1 = max(t0 - dy, 0), min(t1 - dy, BY)
                                out = ps[j % 2][:, b, 0:(t1 - t0) * TROW].rearrange("p (t c) -> p t c", c=TROW)
                                out = out[:, r0 + dy - t0:r1 + dy - t0, IMG * dx:IMG * dx + ROW]
                                mm = pe.matmul(out.rearrange("p t (f b) -> p t f b", f=2),
                                               real(e[:, j, dx, BLK_Y * dy:BLK_Y * (dy + 1), :]
                                                    .rearrange("p y x -> p (y x)")),
                                               real(v[:, k, r0:r1, :, j, :]),
                                               start=m == 0, stop=m == len(parts) - 1, skip_group_check=True)
                            mm.then_inc(mm_done, 1)

        @block.scalar
        def _(act):
            with act.Fori(0, GROUPS) as c:
                act.wait_ge(g_done, c * (PAIRS * GRP * BANKS))
                act.wait_ge(b_loaded, 32)
                act.copy(bias[:, :], b_dw[:, bass.ds(c * GRP, GRP)]).then_inc(bias_here, 1)
                act.wait_ge(bias_here, c + 1)
                for q in range(PAIRS):
                    act.wait_ge(stored[q % 2], (c * (PAIRS // 2) + q // 2) * 16)
                    for j in range(GRP):
                        for b in range(BANKS):
                            act.wait_ge(mm_done, c * (PAIRS * GRP * BANKS) + ((q * GRP + j) * BANKS + b + 1))
                            t0, t1 = CUTS[b] * TROW, CUTS[b + 1] * TROW
                            act.activation(g[:, q % 2, j, t0:t1], ps[j % 2][:, b, 0:t1 - t0], ACT.Gelu,
                                           bias=bias[:, j:j + 1]).then_inc(g_done, 1)


def conv_out(nc, w_out_t, b_out_c, g_dram, y):
    PAIRS = len(g_dram)
    C = g_dram[0].shape[0]
    D = w_out_t.shape[1]
    B, _, H, W = y.shape
    TY, TX = H // BLK_Y, W // BLK_X
    TROW = (TX + 1) * IMG
    ROWN = TX * IMG
    N = TY * ROWN
    KH = C // 128
    XH = BLK_X // 2
    FIRST = BLK_Y - HALO
    ROWS = PAIRS * BLK_Y
    with ExitStack() as ctx:
        n = Named(nc, ctx, "cout")
        w = n.sbuf("w", [128, KH, D])
        whi = n.sbuf("whi", [128, KH, D])
        wlo = n.sbuf("wlo", [128, KH, D])
        bias = n.sbuf("bias", [D, 1])
        graw = n.sbuf("graw", [128, 2, KH, 2, TY * TROW])
        ghi = n.sbuf("ghi", [128, 2, KH, TY, ROWN])
        glo = n.sbuf("glo", [128, 2, KH, TY, ROWN])
        yb = n.sbuf("yb", [D, 2, IMG, TY, W])
        ps = [n.psum(f"ps{i}", [128, 2, BANK]) for i in range(4)]
        w_loaded = n.sem("w_loaded")
        w_split = n.sem("w_split")
        g_loaded = [n.sem(f"g_loaded{i}") for i in range(2)]
        g_hi = n.sem("g_hi")
        g_lo = n.sem("g_lo")
        mm_done = n.sem("mm_done")
        y_act = n.sem("y_act")
        y_dve = n.sem("y_dve")
        stored = [n.sem(f"stored{i}") for i in range(2)]
        block = ctx.enter_context(nc.Block())

        @block.sync
        def _(sp):
            sp.dma_start(w[:], w_out_t.rearrange("(f p) d -> p f d", p=128)).then_inc(w_loaded, 16)
            sp.dma_start(bias[:], b_out_c).then_inc(w_loaded, 16)

            def load(q, r, k, xh, first):
                row = q * BLK_Y + r
                if not first:
                    sp.wait_ge(g_hi, row * BLK_X + (2 * xh - 2))
                    sp.wait_ge(g_lo, row * BLK_X + (2 * xh - 2))
                late = k
                if late:
                    px, t0 = (r - FIRST) * BLK_X + 2 * xh, TROW
                else:
                    px, t0 = (r + HALO) * BLK_X + 2 * xh, 0
                for f in range(KH):
                    sp.dma_start(graw[:, xh % 2, f], g_dram[q][f * 128:(f + 1) * 128, bass.ds(px, 2), t0:t0 + TY * TROW]
                                 ).then_inc(g_loaded[xh % 2], 16)

            def store(q, r, k):
                row = q * BLK_Y + r
                sp.wait_ge(y_act, (row + 1) * BLK_X)
                sp.wait_ge(y_dve, (row + 1) * BLK_X)
                for img in range(IMG):
                    dst = y[bass.ds(q * IMG + img, 1)].rearrange("i d (t s) w -> (i d) t s w", s=BLK_Y)
                    sp.dma_start(dst[:, :, bass.ds(r, 1), :].rearrange("d t s w -> d t (s w)"), yb[:, k, img]
                                 ).then_inc(stored[k], 16)

            def row_step(q, r, k, late, next_row, ahead=True):
                for xh in range(1, XH):
                    load(q, r, late, xh, False)
                if next_row is not None:
                    nq, nr, nlate = next_row
                    load(nq, nr, nlate, 0, False)
                store(q, r, k)

            load(0, 0, 0, 0, True)
            for q in range(PAIRS):
                with sp.Fori(0, FIRST // 2) as i:
                    for k in range(2):
                        row_step(q, i * 2 + k, k, 0, (q, i * 2 + (k + 1), 0))
                for r in range(FIRST // 2 * 2, BLK_Y):
                    nxt = (q, r + 1, int(r + 1 >= FIRST)) if r + 1 < BLK_Y else (q + 1, 0, 0)
                    row_step(q, r, r % 2, int(r >= FIRST), nxt if nxt[0] < PAIRS else None)
            for k in range(2):
                sp.wait_ge(stored[k], 16 * IMG * (ROWS // 2))

        def window(xx, k):
            c0 = IMG if xx < HALO else 0
            return graw[:, xx // 2 % 2, :, xx % 2].rearrange("p f (t c) -> p f t c", c=TROW)[:, :, :, c0:c0 + ROWN]

        def arrived(eng, row, i, k, xx):
            eng.wait_ge(g_loaded[xx // 2 % 2], (row * 2 + (xx // 4 + 1)) * (16 * KH))

        def place(xx, k, half):
            x = (xx - HALO) % BLK_X
            v = yb[:, k].rearrange("p i t (c x) -> p i t c x", x=BLK_X)
            return v[:, :, half * (TY // 2):(half + 1) * (TY // 2), :, x].rearrange("p i t c -> p (t c) i")

        @block.tensor
        def _(pe):
            pe.wait_ge(w_split, 2)
            with pe.Fori(0, ROWS) as row:
                for xx in range(BLK_X):
                    pe.wait_ge(g_hi, row * BLK_X + (xx + 1))
                    pe.wait_ge(g_lo, row * BLK_X + (xx + 1))
                    if xx < 4:
                        pe.wait_ge(y_act, row * BLK_X if xx == 0 else row * BLK_X)
                        pe.wait_ge(y_dve, row * BLK_X if xx == 0 else row * BLK_X)
                    else:
                        pe.wait_ge(y_act, row * BLK_X + (xx - 3))
                        pe.wait_ge(y_dve, row * BLK_X + (xx - 3))
                    for half in range(2):
                        t0, t1 = half * TY // 2, (half + 1) * TY // 2
                        parts = [(f, a, v) for f in range(KH) for a, v in ((whi, ghi), (whi, glo), (wlo, ghi))]
                        for m, (f, a, v) in enumerate(parts):
                            mm = pe.matmul(ps[xx % 4][0:D, half, :], real(a[:, f, :]),
                                           real(v[:, xx % 2, f, t0:t1, :].rearrange("p t c -> p (t c)")),
                                           start=m == 0, stop=m == len(parts) - 1)
                    mm.then_inc(mm_done, 1)

        def used(eng, row, xx):
            if xx >= 2:
                eng.wait_ge(mm_done, row * BLK_X + (xx - 1))
            else:
                eng.wait_ge(mm_done, row * BLK_X)

        @block.scalar
        def _(act):
            def finish(row, i, k, xx):
                act.wait_ge(mm_done, row * BLK_X + (xx + 1))
                act.wait_ge(stored[k], i * (16 * IMG))
                act.activation(place(xx, k, 0), ps[xx % 4][0:D, 0, :].rearrange("p (c i) -> p c i", i=IMG),
                               ACT.Identity, bias=bias[:, 0:1]).then_inc(y_act, 1)

            act.wait_ge(w_loaded, 32)
            with act.Fori(0, ROWS // 2) as i:
                order = [(k, xx) for k in range(2) for xx in range(BLK_X)]
                for m, (k, xx) in enumerate(order):
                    row = i * 2 + k
                    arrived(act, row, i, k, xx)
                    used(act, row, xx)
                    act.copy(real(ghi[:, xx % 2]), window(xx, k)).then_inc(g_hi, 1)
                    if xx:
                        finish(row, i, k, xx - 1)
                    if xx == BLK_X - 1:
                        finish(row, i, k, xx)

        @block.vector
        def _(dve):
            def finish(row, i, k, xx):
                dve.wait_ge(mm_done, row * BLK_X + (xx + 1))
                dve.wait_ge(stored[k], i * (16 * IMG))
                dve.tensor_scalar(place(xx, k, 1), ps[xx % 4][0:D, 1, :].rearrange("p (c i) -> p c i", i=IMG),
                                  bias[:, 0:1], None, ALU.add).then_inc(y_dve, 1)

            dve.wait_ge(w_loaded, 32)
            dve.tensor_copy(real(whi[:]), w[:]).then_inc(w_split, 1)
            dve.wait_ge(w_split, 1)
            dve.tensor_tensor(real(wlo[:]), w[:], whi[:], ALU.subtract).then_inc(w_split, 1)
            with dve.Fori(0, ROWS // 2) as i:
                for k in range(2):
                    for xx in range(BLK_X):
                        row = i * 2 + k
                        dve.wait_ge(g_hi, row * BLK_X + (xx + 1))
                        dve.tensor_tensor(real(glo[:, xx % 2]), window(xx, k), ghi[:, xx % 2], ALU.subtract
                                          ).then_inc(g_lo, 1)
                        if xx:
                            finish(row, i, k, xx - 1)
                        if xx == BLK_X - 1:
                            finish(row, i, k, xx)


def program(nc, x, w_in_t, b_in_r, filt_t, wdw_t, b_dw_r, w_out_t, b_out_c, circ_c, shift_c, y):
    B, D, H, W = x.shape
    C = w_in_t.shape[1]
    PAIRS, BY, BX = B // IMG, H // BLK_Y, W // BLK_X
    e_dram = nc.dram_tensor("composites", [C // GRP, 128, GRP, REACH], F32).ap()
    h_dram = [nc.dram_tensor(f"hidden{q}", [C // GRP, 128, BY, 2, GRP, BX // 2 * IMG], F32).ap() for q in range(PAIRS)]
    g_dram = [nc.dram_tensor(f"gelu{q}", [C, 128, (BY + 1) * (BX + 1) * IMG], F32).ap() for q in range(PAIRS)]
    build_composites(nc, filt_t, wdw_t, circ_c, shift_c, e_dram)
    conv_in(nc, x, w_in_t, h_dram)
    spatial(nc, b_in_r, b_dw_r, e_dram, h_dram, g_dram)
    conv_out(nc, w_out_t, b_out_c, g_dram, y)


def shape_constants():
    ky, kx, xi, u, x = np.ogrid[0:PATCH, 0:PATCH // 2 + 1, 0:PATCH, 0:2 * PATCH, 0:PATCH]
    twice = np.where((kx == 0) | (kx == PATCH // 2), 1.0, 2.0)
    circ = twice * np.cos(2 * np.pi * ((ky * u + kx * (x - xi)) % PATCH) / PATCH) / (PATCH * PATCH)
    i, j, X, u, x = np.ogrid[0:TAPS, 0:TAPS, 0:SPREAD, 0:3 * TAPS, 0:PATCH]
    shift = (u == TAPS + i) & (x == X - (TAPS - 1) + j)
    return (circ.reshape((-1,) + circ.shape[2:]).astype(np.float32),
            shift.reshape((-1,) + shift.shape[2:]).astype(np.float32))


def kernel(x, L0_conv_w_in, L0_conv_b_in, L0_conv_fft_filter, L0_conv_w_dw, L0_conv_b_dw, L0_conv_w_out,
           L0_conv_b_out):
    import concourse.bacc as bacc
    from concourse.bass_utils import run_bass_kernel_spmd

    x = np.ascontiguousarray(x)
    C = L0_conv_w_in.shape[0]
    circ, shift = shape_constants()
    rows = np.ascontiguousarray
    arrays = {
        "x": x,
        "w_in_t": rows(np.asarray(L0_conv_w_in).reshape(C, -1).T),
        "b_in_r": rows(np.asarray(L0_conv_b_in).reshape(1, C)),
        "filt_t": rows(np.asarray(L0_conv_fft_filter).reshape(C, -1).T),
        "wdw_t": rows(np.asarray(L0_conv_w_dw).reshape(C, -1).T),
        "b_dw_r": rows(np.asarray(L0_conv_b_dw).reshape(1, C)),
        "w_out_t": rows(np.asarray(L0_conv_w_out).reshape(-1, C).T),
        "b_out_c": rows(np.asarray(L0_conv_b_out).reshape(-1, 1)),
        "circ_c": circ,
        "shift_c": shift,
    }
    nc = bacc.Bacc("TRN2", target_bir_lowering=False, num_devices=1)
    args = [nc.dram_tensor(name, a.shape, mybir.dt.from_np(a.dtype), kind="ExternalInput").ap()
            for name, a in arrays.items()]
    y = nc.dram_tensor("y", x.shape, F32, kind="ExternalOutput").ap()
    program(nc, *args, y)
    return run_bass_kernel_spmd(nc, [arrays], core_ids=[0]).results[0]["y"]
```

```python
from contextlib import ExitStack

import numpy as np

import concourse.bass as bass
from concourse import mybir
from concourse.alu_op_type import AluOpType as ALU

F32 = mybir.dt.float32
F32R = mybir.dt.float32r
ACT = mybir.ActivationFunctionType

PATCH = 8
TAPS = 7
HALO = TAPS // 2
SPREAD = PATCH + 2 * HALO
BLK_Y, BLK_X = 2 * PATCH, PATCH
PX = BLK_Y * BLK_X
REACH_Y, REACH_X = 2 * BLK_Y, 2 * BLK_X
REACH = REACH_Y * REACH_X
GRP = 4
IMG = 2
BANK = 512
START = 64


def real(ap):
    return ap.bitcast(F32R)


class Named:

    def __init__(self, nc, ctx, stage):
        self.nc, self.ctx, self.stage = nc, ctx, stage

    def sbuf(self, name, shape):
        return self.ctx.enter_context(self.nc.sbuf_tensor(f"{self.stage}_{name}", shape, F32))

    def psum(self, name, shape):
        return self.ctx.enter_context(self.nc.psum_tensor(f"{self.stage}_{name}", shape, F32))

    def sem(self, name):
        sem = self.ctx.enter_context(self.nc.semaphore(f"{self.stage}_{name}"))
        self.nc.gpsimd.sem_inc(sem, START)
        return sem


def build_composites(nc, filt_t, wdw_t, circ_c, shift_c, e_dram):
    freqs, C = filt_t.shape
    taps = wdw_t.shape[0]
    PP = PATCH * PATCH
    SS = SPREAD * SPREAD
    CQ = C // 4
    K_MM = 4 * BANK // C
    D_MM = 4 * BANK // CQ
    K_GROUPS = PP // K_MM
    D_GROUPS = -(-SS // D_MM)
    UNITS = CQ // GRP
    with ExitStack() as ctx:
        n = Named(nc, ctx, "comp")
        filt = n.sbuf("filt", [freqs, C])
        wdw = n.sbuf("wdw", [taps, C])
        circ_tab = n.sbuf("circ_tab", [freqs, PATCH, 2 * PATCH, PATCH])
        shift_tab = n.sbuf("shift_tab", [taps, SPREAD, 3 * TAPS, PATCH])
        circ = n.sbuf("circ", [PP, PP, C])
        shifted = n.sbuf("shifted", [PP, SS, CQ])
        lhs = n.sbuf("lhs", [PP, 2, GRP, 2, PP])
        stage = n.sbuf("stage", [128, 2, GRP, REACH_Y, REACH_X])
        ps = [n.psum(f"ps{i}", [128, 4, BANK]) for i in range(2)]
        loaded = n.sem("loaded")
        zeroed = n.sem("zeroed")
        mm_done = n.sem("mm_done")
        ev_act = n.sem("ev_act")
        ev_dve = n.sem("ev_dve")
        lhs_ready = n.sem("lhs_ready")
        comp_done = n.sem("comp_done")
        top_done = n.sem("top_done")
        bot_done = n.sem("bot_done")
        stored = [n.sem(f"stored{i}") for i in range(2)]
        block = ctx.enter_context(nc.Block())

        table0 = [K_GROUPS + q * D_GROUPS for q in range(4)]

        def groups_by(parity, upto):
            return (upto + 1 - parity) // 2

        def evacuate(eng, t, parity, copy):
            eng.wait_ge(mm_done, START + t + 1)
            if t < K_GROUPS:
                copy(circ[:, t * K_MM:(t + 1) * K_MM, :].rearrange("p a c -> p (a c)"),
                     ps[t % 2][0:PP, :, :].rearrange("p a c -> p (a c)")).then_inc((ev_dve, ev_act)[parity], 1)
            else:
                g = (t - K_GROUPS) % D_GROUPS
                cnt = min(D_MM, SS - g * D_MM)
                copy(shifted[:, g * D_MM:g * D_MM + cnt, :].rearrange("p a c -> p (a c)"),
                     ps[t % 2][0:PP, :, :].rearrange("p a c -> p (a c)")[:, 0:cnt * CQ]
                     ).then_inc((ev_dve, ev_act)[parity], 1)

        @block.sync
        def _(sp):
            sp.dma_start(filt[:], filt_t).then_inc(loaded, 16)
            sp.dma_start(wdw[:], wdw_t).then_inc(loaded, 16)
            sp.dma_start(circ_tab[:], circ_c).then_inc(loaded, 16)
            sp.dma_start(shift_tab[:], shift_c).then_inc(loaded, 16)
            for q in range(4):
                with sp.Fori(0, UNITS // 2) as i:
                    for k in range(2):
                        u = i * 2 + (q * UNITS + k)
                        sp.wait_ge(top_done, u * 2 + (START + 2))
                        sp.wait_ge(bot_done, u * 2 + (START + 2))
                        sp.dma_start(e_dram[u, :, :, :], stage[:, k].rearrange("p c r x -> p c (r x)")
                                     ).then_inc(stored[k], 16)
            for k in range(2):
                sp.wait_ge(stored[k], START + 16 * 2 * UNITS)

        @block.tensor
        def _(pe):
            pe.wait_ge(loaded, START + 64)

            def free(t):
                if t >= 2:
                    pe.wait_ge((ev_dve, ev_act)[t % 2], START + groups_by(t % 2, t - 1))

            for t in range(K_GROUPS):
                free(t)
                for m in range(K_MM):
                    y, x = divmod(t * K_MM + m, PATCH)
                    at = m * C
                    mm = pe.matmul(ps[t % 2][0:PP, at // BANK, at % BANK:at % BANK + C],
                                   circ_tab[:, x, PATCH - y:2 * PATCH - y, :].rearrange("p u v -> p (u v)"), filt[:, :],
                                   start=True, stop=True)
                mm.then_inc(mm_done, 1)
            for q in range(4):
                if q:
                    pe.wait_ge(comp_done, START + q * UNITS)
                    pe.wait_ge(top_done, START + 2 * q * UNITS)
                    pe.wait_ge(bot_done, START + 2 * q * UNITS)
                for g in range(D_GROUPS):
                    t = table0[q] + g
                    free(t)
                    for m in range(min(D_MM, SS - g * D_MM)):
                        Y, X = divmod(g * D_MM + m, SPREAD)
                        at = m * CQ
                        mm = pe.matmul(ps[t % 2][0:PP, at // BANK, at % BANK:at % BANK + CQ],
                                       shift_tab[:, X, SPREAD - 1 - Y:SPREAD - 1 - Y + PATCH, :]
                                       .rearrange("p u v -> p (u v)"),
                                       wdw[:, q * CQ:(q + 1) * CQ], start=True, stop=True)
                    mm.then_inc(mm_done, 1)
                pe.wait_ge(ev_dve, START + groups_by(0, table0[q] + D_GROUPS))
                pe.wait_ge(ev_act, START + groups_by(1, table0[q] + D_GROUPS))
                with pe.Fori(0, UNITS // 2) as i:
                    for k in range(2):
                        u = i * 2 + (q * UNITS + k)
                        pe.wait_ge(lhs_ready, u * 2 + (START + 2))
                        pe.wait_ge(top_done, u * 2 + (START - 2))
                        pe.wait_ge(bot_done, u * 2 + (START - 2))
                        for j in range(GRP):
                            mm = pe.matmul(ps[k][:, j // 2, (j % 2) * SS:(j % 2 + 1) * SS],
                                           lhs[:, k, j].rearrange("p h a -> p (h a)"),
                                           shifted[:, :, bass.ds(i * (2 * GRP) + (k * GRP + j), 1)]
                                           .rearrange("p a c -> p (a c)"),
                                           start=True, stop=True)
                        mm.then_inc(comp_done, 1)

        def composites(eng, q, part, done, copy, before):
            rows = slice(0, PP) if part == 0 else slice(PP, 128)
            r0 = PATCH * part
            with eng.Fori(0, UNITS // 2) as i:
                for k in range(2):
                    u = i * 2 + (q * UNITS + k)
                    before(i, k, u)
                    eng.wait_ge(comp_done, u + (START + 1))
                    eng.wait_ge(stored[k], i * 16 + (START + q * UNITS // 2 * 16))
                    for b in range(GRP // 2):
                        src = ps[k][rows, b, 0:2 * SS].rearrange("p (c r x) -> p c r x", c=2, x=SPREAD)
                        if part == 0:
                            copy(stage[rows, k, 2 * b:2 * b + 2, BLK_Y:PATCH + SPREAD, 0:SPREAD],
                                 src[:, :, PATCH:SPREAD, :])
                        copy(stage[rows, k, 2 * b:2 * b + 2, r0:r0 + SPREAD, 0:SPREAD], src).then_inc(done, 1)

        @block.scalar
        def _(act):
            act.wait_ge(zeroed, START + 1)
            for t in range(1, K_GROUPS, 2):
                evacuate(act, t, 1, act.copy)
            for q in range(4):
                for t in range(table0[q], table0[q] + D_GROUPS):
                    if t % 2 == 1:
                        evacuate(act, t, 1, act.copy)
                composites(act, q, 0, top_done, act.copy, lambda i, k, u: None)

        @block.vector
        def _(dve):
            dve.memset(stage[:], 0.0).then_inc(zeroed, 1)
            dve.wait_ge(zeroed, START + 1)
            for t in range(0, K_GROUPS, 2):
                evacuate(dve, t, 0, dve.tensor_copy)
            for q in range(4):
                for t in range(table0[q], table0[q] + D_GROUPS):
                    if t % 2 == 0:
                        evacuate(dve, t, 0, dve.tensor_copy)
                dve.wait_ge(ev_dve, START + groups_by(0, K_GROUPS))
                dve.wait_ge(ev_act, START + groups_by(1, K_GROUPS))

                def pick(i, k, u):
                    dve.wait_ge(comp_done, u + (START - 1))
                    for half in range(2):
                        dve.tensor_copy(lhs[:, k, :, half, :],
                                        circ[:, :, bass.ds(i * (2 * GRP) + (q * CQ + k * GRP), GRP)]
                                        .rearrange("p a c -> p c a")).then_inc(lhs_ready, 1)

                composites(dve, q, 1, bot_done, dve.tensor_copy, pick)


class ConvIn:

    def __init__(self, n, x, w_in_t, pair0, h_dram, banks, evacuators, slots):
        self.x, self.w_in_t, self.pair0 = x, w_in_t, pair0
        self.h_view = [h.rearrange("g p y f j b -> y f p g (j b)") for h in h_dram]
        self.C = C = w_in_t.shape[1]
        self.D = w_in_t.shape[0]
        self.HW = x.shape[3] // 2
        self.SETS = self.HW // BLK_X
        self.banks, self.slots = banks, slots
        self.xs = n.sbuf("xs", [128, slots, BLK_Y, self.HW])
        self.xsplit = n.sbuf("xsplit", [128, slots, IMG, self.SETS, PX])
        self.hs = n.sbuf("hs", [128, slots, C, self.SETS * IMG])
        self.w = n.sbuf("w_in", [128, C])
        self.whi = n.sbuf("w_in_hi", [128, C])
        self.wlo = n.sbuf("w_in_lo", [128, C])
        self.w_loaded = n.sem("w_in_loaded")
        self.w_split = n.sem("w_in_split")
        self.x_loaded = [n.sem(f"x_loaded{i}") for i in range(slots)]
        self.x_hi = n.sem("x_hi")
        self.x_lo = n.sem("x_lo")
        self.mm_done = n.sem("hidden_mm")
        self.ev = [n.sem(f"hidden_ev_{e}") for e in evacuators]
        self.stored = [n.sem(f"hidden_stored{i}") for i in range(slots)]

    def slot(self, f):
        return f % self.slots

    def before(self, ab, u):
        return ab if self.slots == 2 else u

    def load_w(self, sp):
        for half in range(2):
            sp.dma_start(self.w[64 * half:64 * half + self.D, :], self.w_in_t).then_inc(self.w_loaded, 16)

    def split_w(self, dve):
        dve.wait_ge(self.w_loaded, START + 32)
        dve.tensor_copy(real(self.whi[:, :]), self.w[:, :]).then_inc(self.w_split, 1)
        dve.wait_ge(self.w_split, START + 1)
        dve.tensor_tensor(real(self.wlo[:, :]), self.w[:, :], self.whi[:, :], ALU.subtract).then_inc(self.w_split, 1)

    def load(self, sp, a, b, f, u):
        sp.wait_ge(self.x_hi, u * IMG + (START - IMG * (self.slots - 1)))
        sp.wait_ge(self.x_lo, u * IMG + (START - IMG * (self.slots - 1)))
        q = (self.pair0 + a) * IMG
        src = self.x[q:q + IMG, :, bass.ds(b * BLK_Y, BLK_Y), f * self.HW:(f + 1) * self.HW]
        sp.dma_start(self.xs[:, self.slot(f)], src.rearrange("i c r w -> (i c) r w")
                     ).then_inc(self.x_loaded[self.slot(f)], 16)

    def store(self, sp, a, b, f, u):
        for ev in self.ev:
            sp.wait_ge(ev, u * (self.SETS // len(self.ev)) + (START + self.SETS // len(self.ev)))
        half = self.C // 2
        for c0 in range(0, self.C, half):
            sp.dma_start(self.h_view[a][b, f, :, c0 // GRP:(c0 + half) // GRP, :],
                         self.hs[:, self.slot(f), c0:c0 + half, :].rearrange("p (g j) b -> p g (j b)", j=GRP)
                         ).then_inc(self.stored[self.slot(f)], 16)

    def stored_all(self, sp, units):
        for sem in self.stored:
            sp.wait_ge(sem, START + 32 * units // self.slots)

    def _images(self, eng, ab, f, u):
        k = self.slot(f)
        eng.wait_ge(self.x_loaded[k], self.before(ab, u) * 16 + (START + 16))
        eng.wait_ge(self.mm_done, u * self.SETS + (START - self.SETS * (self.slots - 1)))
        for img in range(IMG):
            own, other = slice(64 * img, 64 * img + 64), slice(64 - 64 * img, 128 - 64 * img)
            blocks = self.xsplit[:, k, img].rearrange("p b (r x) -> p r b x", x=BLK_X)
            raw = self.xs[own, k].rearrange("p r (b x) -> p r b x", x=BLK_X)
            yield img, raw, blocks[own], blocks[other]

    def split_hi(self, act, ab, f, u):
        for img, raw, hi, lo in self._images(act, ab, f, u):
            act.copy(real(hi), raw).then_inc(self.x_hi, 1)

    def split_lo(self, dve, ab, f, u):
        for img, raw, hi, lo in self._images(dve, ab, f, u):
            dve.wait_ge(self.x_hi, u * IMG + (START + 1 + img))
            dve.tensor_tensor(real(lo), raw, hi, ALU.subtract).then_inc(self.x_lo, 1)

    def products(self, pe, f, u, m):
        if m == 0:
            pe.wait_ge(self.x_lo, u * IMG + (START + IMG))
        E, NB = len(self.ev), len(self.banks)
        pe.wait_ge(self.ev[m % E], u * (self.SETS // E) + (START + (m - NB) // E + 1))
        for img in range(IMG):
            out = self.banks[m % NB][:, img * self.C:(img + 1) * self.C]
            lhs = real(self.xsplit[:, self.slot(f), img, m, :])
            pe.matmul(out, lhs, real(self.whi[:, :]), start=True, stop=False)
            mm = pe.matmul(out, lhs, real(self.wlo[:, :]), start=False, stop=True)
        mm.then_inc(self.mm_done, 1)

    def evacuate(self, eng, copy, ab, f, u, m):
        if m < len(self.ev):
            eng.wait_ge(self.stored[self.slot(f)], self.before(ab, u) * 32 + START)
        eng.wait_ge(self.mm_done, u * self.SETS + (START + m + 1))
        copy(self.hs[:, self.slot(f), :, IMG * m:IMG * (m + 1)],
             self.banks[m % len(self.banks)].rearrange("p (i c) -> p c i", i=IMG)
             ).then_inc(self.ev[m % len(self.ev)], 1)


class Spatial:

    def __init__(self, n, b_in_r, b_dw_r, e_dram, h_dram, g_dram):
        self.PAIRS = len(h_dram)
        self.GROUPS, _, self.BY, _, _, self.HALF = h_dram[0].shape
        self.C = C = self.GROUPS * GRP
        self.ROW = 2 * self.HALF
        self.TY, self.TROW = self.BY + 1, self.ROW + IMG
        self.CUTS = [0, 6, 12, self.TY]
        self.BANKS = len(self.CUTS) - 1
        self.b_in_r, self.b_dw_r, self.e_dram, self.h_dram, self.g_dram = b_in_r, b_dw_r, e_dram, h_dram, g_dram
        assert self.PAIRS == 2
        self.b_in = n.sbuf("b_in", [128, C])
        self.b_dw = n.sbuf("b_dw", [128, C])
        self.bias = n.sbuf("bias", [128, GRP])
        self.eraw = n.sbuf("eraw", [128, GRP, REACH_Y, 2, BLK_X])
        self.ehi = n.sbuf("ehi", [128, GRP, 2, REACH_Y, BLK_X])
        self.elo = n.sbuf("elo", [128, GRP, 2, REACH_Y, BLK_X])
        self.h = n.sbuf("h", [128, self.PAIRS, self.BY, 2, GRP, self.HALF])
        self.hi = n.sbuf("hi", [128, GRP, self.BY, 2, self.HALF])
        self.low = n.sbuf("low", [128, GRP, self.BY, 2, self.HALF])
        self.g = n.sbuf("g", [128, GRP, self.TY * self.TROW])
        self.ps = [n.psum(f"ps{i}", [128, self.BANKS, BANK]) for i in range(2)]
        self.b_loaded = n.sem("b_loaded")
        self.bias_here = n.sem("bias_here")
        self.e_loaded = n.sem("e_loaded")
        self.h_loaded = [n.sem(f"h_loaded{i}") for i in range(self.PAIRS)]
        self.e_hi = n.sem("e_hi")
        self.e_lo = n.sem("e_lo")
        self.h_hi = n.sem("h_hi")
        self.h_lo = n.sem("h_lo")
        self.h_low = n.sem("h_low")
        self.mm_done = n.sem("mm_done")
        self.g_done = n.sem("g_done")
        self.stored = [n.sem(f"g_stored{i}") for i in range(GRP)]
        self.PER = self.PAIRS * GRP


    def load_biases(self, sp):
        for t, src in ((self.b_in, self.b_in_r), (self.b_dw, self.b_dw_r)):
            sp.dma_start(t[:], src.to_broadcast([128, self.C])).then_inc(self.b_loaded, 16)

    def load_e(self, sp, c):
        sp.wait_ge(self.e_lo, c * GRP + START)
        sp.dma_start(self.eraw[:].rearrange("p c r d x -> p c (r d x)"), self.e_dram[c]).then_inc(self.e_loaded, 16)

    def load_h(self, sp, c, q):
        sp.wait_ge(self.mm_done, c * (self.PER * self.BANKS) + (START + (q * GRP + GRP - self.PER) * self.BANKS))
        sp.dma_start(self.h[:, q].rearrange("p y f j b -> p (y f j b)"),
                     self.h_dram[q][c].rearrange("p y f j b -> p (y f j b)")).then_inc(self.h_loaded[q], 16)

    def store(self, sp, c, q, j):
        sp.wait_ge(self.g_done, c * (self.PER * self.BANKS) + (START + (q * GRP + j + 1) * self.BANKS))
        sp.dma_start(self.g_dram[q][bass.ds(c * GRP + j, 1)].rearrange("j p t -> (j p) t"), self.g[:, j]
                     ).then_inc(self.stored[j], 16)

    def stored_all(self, sp):
        for sem in self.stored:
            sp.wait_ge(sem, START + 16 * self.PAIRS * self.GROUPS)

    def split(self, dve, c, q, j):
        w = q * GRP + j
        if w == 0:
            dve.wait_ge(self.b_loaded, START + 32)
        if j == 0:
            dve.wait_ge(self.h_loaded[q], c * 16 + (START + 16))
        raw = self.h[:, q, :, :, j, :].rearrange("p y f b -> p (y f) b")
        big = self.hi[:, j].rearrange("p y f b -> p (y f) b")
        low = self.low[:, j].rearrange("p y f b -> p (y f) b")
        bias = self.b_in[:, bass.ds(c * GRP + j, 1)]
        dve.wait_ge(self.mm_done, c * (self.PER * self.BANKS) + (START + (w - GRP + 1) * self.BANKS))
        dve.tensor_scalar(real(big), raw, bias, None, ALU.add).then_inc(self.h_hi, 1)
        dve.wait_ge(self.h_hi, c * self.PER + (START + w + 1))
        dve.scalar_tensor_tensor(real(raw), raw, bias, big, ALU.add, ALU.subtract).then_inc(self.h_lo, 1)
        dve.tensor_copy(real(low[64:128]), big[64:128]).then_inc(self.h_low, 1)
        dve.wait_ge(self.h_lo, c * self.PER + (START + w + 1))
        dve.tensor_copy(real(low[0:64]), raw[64:128]).then_inc(self.h_low, 1)
        if q == 0:
            if j == 0:
                dve.wait_ge(self.e_loaded, c * 16 + (START + 16))
            eraw = self.eraw[:, j].rearrange("p r d x -> p d r x")
            dve.tensor_copy(real(self.ehi[:, j]), eraw).then_inc(self.e_hi, 1)
            dve.wait_ge(self.e_hi, c * GRP + (START + j + 1))
            dve.tensor_tensor(real(self.elo[:, j]), eraw, self.ehi[:, j], ALU.subtract).then_inc(self.e_lo, 1)

    def products(self, pe, c, q, j, between):
        w = q * GRP + j
        pe.wait_ge(self.h_low, c * (2 * self.PER) + (START + 2 * (w + 1)))
        if q == 0:
            pe.wait_ge(self.e_lo, c * GRP + (START + j + 1))
        for b in range(self.BANKS):
            pe.wait_ge(self.g_done, c * (self.PER * self.BANKS) + (START + (w - 2) * self.BANKS + b + 1))
            t0, t1 = self.CUTS[b], self.CUTS[b + 1]
            lo = self.h[:, q, :, :, j, :]
            parts = [(0, dx, e, v) for dx in range(2)
                     for e, v in ((self.ehi, self.hi[:, j]), (self.ehi, lo), (self.elo, self.hi[:, j]))]
            parts += [(1, dx, e, self.low[:, j]) for dx in range(2) for e in (self.ehi, self.elo)]
            for m, (dy, dx, e, v) in enumerate(parts):
                r0, r1 = max(t0 - dy, 0), min(t1 - dy, self.BY)
                out = self.ps[j % 2][:, b, 0:(t1 - t0) * self.TROW].rearrange("p (t c) -> p t c", c=self.TROW)
                out = out[:, r0 + dy - t0:r1 + dy - t0, IMG * dx:IMG * dx + self.ROW]
                mm = pe.matmul(out.rearrange("p t (f b) -> p t f b", f=2),
                               real(e[:, j, dx, BLK_Y * dy:BLK_Y * (dy + 1), :].rearrange("p y x -> p (y x)")),
                               real(v[:, r0:r1]), start=m == 0, stop=m == len(parts) - 1, skip_group_check=True)
            mm.then_inc(self.mm_done, 1)
            between(b)

    def biases(self, act, c):
        act.wait_ge(self.g_done, c * (self.PER * self.BANKS) + START)
        act.wait_ge(self.b_loaded, START + 32)
        act.copy(self.bias[:, :], self.b_dw[:, bass.ds(c * GRP, GRP)]).then_inc(self.bias_here, 1)
        act.wait_ge(self.bias_here, c + (START + 1))

    def gelu(self, act, c, q, j, b):
        w = q * GRP + j
        if b == 0:
            act.wait_ge(self.stored[j], c * (16 * self.PAIRS) + (START + 16 * q))
        act.wait_ge(self.mm_done, c * (self.PER * self.BANKS) + (START + w * self.BANKS + b + 1))
        t0, t1 = self.CUTS[b] * self.TROW, self.CUTS[b + 1] * self.TROW
        act.activation(self.g[:, j, t0:t1], self.ps[j % 2][:, b, 0:t1 - t0], ACT.Gelu, bias=self.bias[:, j:j + 1]
                       ).then_inc(self.g_done, 1)


class ConvOut:

    def __init__(self, n, w_out_t, b_out_c, pair0, g_dram, y, banks, evacuators, slots, y_slots):
        self.w_out_t, self.b_out_c, self.pair0, self.g_dram, self.y = w_out_t, b_out_c, pair0, g_dram, y
        self.C, self.D = w_out_t.shape
        self.KH = KH = self.C // 128
        H, W = y.shape[2:]
        self.TY, self.TX = H // BLK_Y, W // BLK_X
        self.TROW, self.ROWN = (self.TX + 1) * IMG, self.TX * IMG
        self.banks, self.slots, self.y_slots = banks, slots, y_slots
        self.w = n.sbuf("w_out", [128, KH, self.D])
        self.whi = n.sbuf("w_out_hi", [128, KH, self.D])
        self.wlo = n.sbuf("w_out_lo", [128, KH, self.D])
        self.bias = n.sbuf("b_out", [self.D, 1])
        self.graw = n.sbuf("graw", [128, slots, KH, self.TY * self.TROW])
        self.ghi = n.sbuf("ghi", [128, 2, KH, self.TY, self.ROWN])
        self.yb = n.sbuf("yb", [self.D, y_slots, IMG, self.TY, W])
        self.w_loaded = n.sem("w_out_loaded")
        self.w_split = n.sem("w_out_split")
        self.g_loaded = [n.sem(f"g_loaded{i}") for i in range(slots)]
        self.g_hi = n.sem("g_hi")
        self.g_lo = n.sem("g_lo")
        self.mm_done = n.sem("y_mm")
        self.ev = [n.sem(f"y_ev_{e}") for e in evacuators]
        self.stored = [n.sem(f"y_stored{i}") for i in range(y_slots)]

    def load_w(self, sp):
        sp.dma_start(self.w[:], self.w_out_t.rearrange("(f p) d -> p f d", p=128)).then_inc(self.w_loaded, 16)
        sp.dma_start(self.bias[:], self.b_out_c).then_inc(self.w_loaded, 16)

    def split_w(self, dve):
        dve.wait_ge(self.w_loaded, START + 32)
        dve.tensor_copy(real(self.whi[:]), self.w[:]).then_inc(self.w_split, 1)
        dve.wait_ge(self.w_split, START + 1)
        dve.tensor_tensor(real(self.wlo[:]), self.w[:], self.whi[:], ALU.subtract).then_inc(self.w_split, 1)

    def load(self, sp, a, r, late, xx):
        k = xx % self.slots
        sp.wait_ge(self.mm_done, (r + a * BLK_Y) * (2 * BLK_X) + (START + 2 * (xx + 1 - self.slots)))
        px = (r + (HALO - BLK_Y if late else HALO)) * BLK_X + xx
        t0 = self.TROW if late else 0
        for f in range(self.KH):
            sp.dma_start(self.graw[:, k, f], self.g_dram[a][f * 128:(f + 1) * 128, bass.ds(px, 1), t0:t0 + self.TY * self.TROW]
                         .rearrange("c x t -> c (x t)")).then_inc(self.g_loaded[k], 16)

    def store(self, sp, a, r, k):
        for ev in self.ev:
            per = 2 * BLK_X // len(self.ev)
            sp.wait_ge(ev, (r + a * BLK_Y) * per + (START + per))
        k = k % self.y_slots
        for img in range(IMG):
            dst = self.y[(self.pair0 + a) * IMG + img].rearrange("d (t s) w -> d t s w", s=BLK_Y)
            sp.dma_start(dst[:, :, bass.ds(r, 1), :].rearrange("d t s w -> d t (s w)"), self.yb[:, k, img]
                         ).then_inc(self.stored[k], 16)

    def stored_all(self, sp, rows):
        for sem in self.stored:
            sp.wait_ge(sem, START + 16 * IMG * rows // self.y_slots)

    def _window(self, k, xx):
        c0 = IMG if xx < HALO else 0
        return self.graw[:, k].rearrange("p f (t c) -> p f t c", c=self.TROW)[:, :, :, c0:c0 + self.ROWN]

    def split_hi(self, act, row, xx):
        k = xx % self.slots
        act.wait_ge(self.g_loaded[k], row * (BLK_X // self.slots * 16 * self.KH) + (START + (xx // self.slots + 1) * 16 * self.KH))
        act.wait_ge(self.mm_done, row * (2 * BLK_X) + (START + 2 * (xx - 1)))
        act.copy(real(self.ghi[:, xx % 2]), self._window(k, xx)).then_inc(self.g_hi, 1)

    def split_lo(self, dve, row, xx):
        v = self._window(xx % self.slots, xx)
        dve.wait_ge(self.g_hi, row * BLK_X + (START + xx + 1))
        dve.tensor_tensor(real(v), v, self.ghi[:, xx % 2], ALU.subtract).then_inc(self.g_lo, 1)

    def products(self, pe, row, xx, half):
        NB, E = len(self.banks), len(self.ev)
        m = 2 * xx + half
        if half == 0:
            pe.wait_ge(self.g_lo, row * BLK_X + (START + xx + 1))
        pe.wait_ge(self.ev[m % E], row * (2 * BLK_X // E) + (START + (m - NB) // E + 1))
        t0, t1 = half * self.TY // 2, (half + 1) * self.TY // 2
        lo = self._window(xx % self.slots, xx)
        hi = self.ghi[:, xx % 2]
        parts = [(f, a, v) for f in range(self.KH) for a, v in ((self.whi, hi), (self.whi, lo), (self.wlo, hi))]
        for i, (f, a, v) in enumerate(parts):
            mm = pe.matmul(self.banks[m % NB][0:self.D, :].rearrange("p (t c) -> p t c", c=self.ROWN),
                           real(a[:, f, :]), real(v[:, f, t0:t1, :]), start=i == 0, stop=i == len(parts) - 1)
        mm.then_inc(self.mm_done, 1)

    def evacuate(self, eng, row, i, k, xx, half):
        m = 2 * xx + half
        if xx == 0:
            eng.wait_ge(self.stored[k % self.y_slots], (i if self.y_slots == 2 else row) * (16 * IMG) + START)
        eng.wait_ge(self.mm_done, row * (2 * BLK_X) + (START + m + 1))
        x = (xx - HALO) % BLK_X
        out = self.yb[:, k % self.y_slots].rearrange("p i t (c x) -> p i t c x", x=BLK_X)
        out = out[:, :, half * (self.TY // 2):(half + 1) * (self.TY // 2), :, x].rearrange("p i t c -> p (t c) i")
        src = self.banks[m % len(self.banks)][0:self.D, :].rearrange("p (c i) -> p c i", i=IMG)
        if m % len(self.ev) == 0:
            eng.activation(out, src, ACT.Identity, bias=self.bias[:, 0:1]).then_inc(self.ev[0], 1)
        else:
            eng.tensor_scalar(out, src, self.bias[:, 0:1], None, ALU.add).then_inc(self.ev[1], 1)


def conv_in_alone(nc, x, w_in_t, pair0, h_dram):
    STRIPS = x.shape[2] // BLK_Y
    with ExitStack() as ctx:
        n = Named(nc, ctx, f"cin{pair0}")
        ps = n.psum("ps", [128, 8, BANK])
        cin = ConvIn(n, x, w_in_t, pair0, h_dram, [ps[:, i] for i in range(8)], ["act", "dve"], 2)
        block = ctx.enter_context(nc.Block())

        @block.sync
        def _(sp):
            cin.load_w(sp)
            for f in range(2):
                cin.load(sp, 0, 0, f, f)
            for a in range(2):
                def strip(b, last):
                    for f in range(2):
                        u = b * 2 + (a * (2 * STRIPS) + f)
                        if not last:
                            cin.load(sp, a, b + 1, f, u + 2)
                        elif a == 0:
                            cin.load(sp, 1, 0, f, u + 2)
                        cin.store(sp, a, b, f, u)
                with sp.Fori(0, STRIPS - 1) as b:
                    strip(b, False)
                strip(STRIPS - 1, True)
            cin.stored_all(sp, 4 * STRIPS)

        @block.tensor
        def _(pe):
            pe.wait_ge(cin.w_split, START + 2)
            with pe.Fori(0, 2 * STRIPS) as ab:
                for f in range(2):
                    for m in range(cin.SETS):
                        cin.products(pe, f, ab * 2 + f, m)

        @block.scalar
        def _(act):
            cin.split_hi(act, 0, 0, 0)

            def strip(ab, last):
                cin.split_hi(act, ab, 1, ab * 2 + 1)
                for m in range(0, cin.SETS, 2):
                    cin.evacuate(act, act.copy, ab, 0, ab * 2, m)
                if not last:
                    cin.split_hi(act, ab + 1, 0, ab * 2 + 2)
                for m in range(0, cin.SETS, 2):
                    cin.evacuate(act, act.copy, ab, 1, ab * 2 + 1, m)
            with act.Fori(0, 2 * STRIPS - 1) as ab:
                strip(ab, False)
            strip(2 * STRIPS - 1, True)

        @block.vector
        def _(dve):
            cin.split_w(dve)
            cin.split_lo(dve, 0, 0, 0)

            def strip(ab, last):
                cin.split_lo(dve, ab, 1, ab * 2 + 1)
                for m in range(1, cin.SETS, 2):
                    cin.evacuate(dve, dve.tensor_copy, ab, 0, ab * 2, m)
                if not last:
                    cin.split_lo(dve, ab + 1, 0, ab * 2 + 2)
                for m in range(1, cin.SETS, 2):
                    cin.evacuate(dve, dve.tensor_copy, ab, 1, ab * 2 + 1, m)
            with dve.Fori(0, 2 * STRIPS - 1) as ab:
                strip(ab, False)
            strip(2 * STRIPS - 1, True)


def spatial_beside_conv_in(nc, b_in_r, b_dw_r, e_dram, h_dram, g_dram, x, w_in_t, pair0, h_next):
    with ExitStack() as ctx:
        n = Named(nc, ctx, "sci")
        sp_ = Spatial(n, b_in_r, b_dw_r, e_dram, h_dram, g_dram)
        ps = n.psum("psx", [128, 2, BANK])
        cin = ConvIn(n, x, w_in_t, pair0, h_next, [ps[:, i] for i in range(2)], ["act"], 1)
        block = ctx.enter_context(nc.Block())
        STRIPS = x.shape[2] // BLK_Y
        places = [(w, b) for w in range(2, 8) for b in range(3)][:cin.SETS]

        @block.sync
        def _(sp):
            sp_.load_biases(sp)
            cin.load_w(sp)
            sp_.load_e(sp, 0)
            sp_.load_h(sp, 0, 0)
            cin.load(sp, 0, 0, 0, 0)
            for a in range(2):
                def group(b, k, last):
                    c = b * 2 + (a * 2 * STRIPS + k)
                    sp_.load_h(sp, c, 1)
                    for j in range(GRP):
                        sp_.store(sp, c, 0, j)
                        if j == 0 and not (last and a == 1):
                            if k == 0:
                                cin.load(sp, a, b, 1, c + 1)
                            elif not last:
                                cin.load(sp, a, b + 1, 0, c + 1)
                            else:
                                cin.load(sp, 1, 0, 0, c + 1)
                    if not (last and a == 1):
                        sp_.load_e(sp, c + 1)
                        sp_.load_h(sp, c + 1, 0)
                    for j in range(GRP):
                        if j == GRP - 1:
                            cin.store(sp, a, b, k, c)
                        sp_.store(sp, c, 1, j)
                with sp.Fori(0, STRIPS - 1) as b:
                    group(b, 0, False)
                    group(b, 1, False)
                group(STRIPS - 1, 0, False)
                group(STRIPS - 1, 1, True)
            sp_.stored_all(sp)
            cin.stored_all(sp, sp_.GROUPS)

        @block.tensor
        def _(pe):
            pe.wait_ge(cin.w_split, START + 2)
            with pe.Fori(0, sp_.GROUPS // 2) as ab:
                for k in range(2):
                    c = ab * 2 + k
                    for w in range(sp_.PER):
                        def between(b):
                            if (w, b) in places:
                                cin.products(pe, k, c, places.index((w, b)))
                        sp_.products(pe, c, w // GRP, w % GRP, between)

        @block.scalar
        def _(act):
            with act.Fori(0, sp_.GROUPS // 2) as ab:
                for k in range(2):
                    c = ab * 2 + k
                    cin.split_hi(act, ab, k, c)
                    sp_.biases(act, c)
                    for w in range(sp_.PER):
                        for b in range(sp_.BANKS):
                            sp_.gelu(act, c, w // GRP, w % GRP, b)
                            if (w, b) in places:
                                cin.evacuate(act, act.copy, ab, k, c, places.index((w, b)))

        @block.vector
        def _(dve):
            cin.split_w(dve)
            with dve.Fori(0, sp_.GROUPS // 2) as ab:
                for k in range(2):
                    c = ab * 2 + k
                    for w in range(sp_.PER):
                        sp_.split(dve, c, w // GRP, w % GRP)
                        if w == GRP - 1:
                            cin.split_lo(dve, ab, k, c)


def spatial_beside_conv_out(nc, b_in_r, b_dw_r, e_dram, h_dram, g_dram, w_out_t, b_out_c, pair0, g_before, y):
    with ExitStack() as ctx:
        n = Named(nc, ctx, "sco")
        sp_ = Spatial(n, b_in_r, b_dw_r, e_dram, h_dram, g_dram)
        ps = n.psum("psy", [128, 2, BANK])
        out = ConvOut(n, w_out_t, b_out_c, pair0, g_before, y, [ps[:, i] for i in range(2)], ["act"], 4, 1)
        block = ctx.enter_context(nc.Block())
        FIRST = BLK_Y - HALO
        places = [(1, 2), (2, 2), (3, 2), (4, 2), (5, 0), (5, 2), (6, 2), (7, 2)]
        hi_at = {0: [0], 2: [1], 4: [2], 5: [3]}
        lo_at = {3: [0], 5: [1], 7: [2, 3]}

        @block.sync
        def _(sp):
            sp_.load_biases(sp)
            out.load_w(sp)
            sp_.load_e(sp, 0)
            sp_.load_h(sp, 0, 0)
            for xx in range(4):
                out.load(sp, 0, 0, 0, xx)
            for a in range(2):
                def group(b, k):
                    still = isinstance(b, int)
                    last = still and b == BLK_Y - 1 and k == 1
                    c = b * 2 + (a * 2 * BLK_Y + k)
                    sp_.load_h(sp, c, 1)
                    for w in range(sp_.PER):
                        if w == GRP and not (last and a == 1):
                            sp_.load_e(sp, c + 1)
                            sp_.load_h(sp, c + 1, 0)
                        if w in (3, 5, 6):
                            ahead(b, k, {3: 0, 5: 1, 6: 2}[w], still)
                        sp_.store(sp, c, w // GRP, w % GRP)
                    if not (last and a == 1):
                        ahead(b, k, 3, still)
                    if k == 1:
                        out.store(sp, a, b, 0)

                def ahead(b, k, m, still):
                    xx = 4 * k + m + 4
                    if xx < BLK_X:
                        out.load(sp, a, b, int(still and b >= FIRST), xx)
                    elif not still or b + 1 < BLK_Y:
                        out.load(sp, a, b + 1, int(still and b + 1 >= FIRST), xx - BLK_X)
                    elif a == 0:
                        out.load(sp, 1, 0, 0, xx - BLK_X)

                with sp.Fori(0, FIRST - 1) as b:
                    for k in range(2):
                        group(b, k)
                for b in range(FIRST - 1, BLK_Y):
                    for k in range(2):
                        group(b, k)
            sp_.stored_all(sp)
            out.stored_all(sp, 2 * BLK_Y)

        @block.tensor
        def _(pe):
            pe.wait_ge(out.w_split, START + 2)
            with pe.Fori(0, sp_.GROUPS // 2) as row:
                for k in range(2):
                    c = row * 2 + k
                    for w in range(sp_.PER):
                        def between(b):
                            if (w, b) in places:
                                m = places.index((w, b))
                                out.products(pe, row, 4 * k + m // 2, m % 2)
                        sp_.products(pe, c, w // GRP, w % GRP, between)

        @block.scalar
        def _(act):
            act.wait_ge(out.w_loaded, START + 32)
            with act.Fori(0, sp_.GROUPS // 2) as row:
                for k in range(2):
                    c = row * 2 + k
                    sp_.biases(act, c)
                    for w in range(sp_.PER):
                        for m in hi_at.get(w, []):
                            out.split_hi(act, row, 4 * k + m)
                        for b in range(sp_.BANKS):
                            sp_.gelu(act, c, w // GRP, w % GRP, b)
                            if (w, b) in places:
                                m = places.index((w, b))
                                out.evacuate(act, row, None, 0, 4 * k + m // 2, m % 2)

        @block.vector
        def _(dve):
            out.split_w(dve)
            with dve.Fori(0, sp_.GROUPS // 2) as row:
                for k in range(2):
                    c = row * 2 + k
                    for w in range(sp_.PER):
                        sp_.split(dve, c, w // GRP, w % GRP)
                        for m in lo_at.get(w, []):
                            out.split_lo(dve, row, 4 * k + m)


def conv_out_alone(nc, w_out_t, b_out_c, pair0, g_dram, y):
    ROWS = 2 * BLK_Y
    with ExitStack() as ctx:
        n = Named(nc, ctx, "cout")
        ps = n.psum("ps", [128, 8, BANK])
        out = ConvOut(n, w_out_t, b_out_c, pair0, g_dram, y, [ps[:, i] for i in range(8)], ["act", "dve"], 8, 2)
        block = ctx.enter_context(nc.Block())
        FIRST = BLK_Y - HALO

        @block.sync
        def _(sp):
            out.load_w(sp)
            for xx in range(BLK_X):
                out.load(sp, 0, 0, 0, xx)
            for a in range(2):
                def row_step(r, k):
                    for xx in range(BLK_X):
                        if not isinstance(r, int) or r + 1 < BLK_Y:
                            out.load(sp, a, r + 1, int(isinstance(r, int) and r + 1 >= FIRST), xx)
                        elif a == 0:
                            out.load(sp, 1, 0, 0, xx)
                    out.store(sp, a, r, k)
                with sp.Fori(0, FIRST // 2) as i:
                    for k in range(2):
                        row_step(i * 2 + k, k)
                for r in range(FIRST // 2 * 2, BLK_Y):
                    row_step(r, r % 2)
            out.stored_all(sp, ROWS)

        @block.tensor
        def _(pe):
            pe.wait_ge(out.w_split, START + 2)
            with pe.Fori(0, ROWS) as row:
                for xx in range(BLK_X):
                    for half in range(2):
                        out.products(pe, row, xx, half)

        def columns(i, one, finish):
            order = [(k, xx) for k in range(2) for xx in range(BLK_X)]
            for m, (k, xx) in enumerate(order):
                one(i * 2 + k, xx)
                if m:
                    k, xx = order[m - 1]
                    finish(i * 2 + k, k, xx)
            k, xx = order[-1]
            finish(i * 2 + k, k, xx)

        @block.scalar
        def _(act):
            act.wait_ge(out.w_loaded, START + 32)
            with act.Fori(0, ROWS // 2) as i:
                columns(i, lambda row, xx: out.split_hi(act, row, xx),
                        lambda row, k, xx: out.evacuate(act, row, i, k, xx, 0))

        @block.vector
        def _(dve):
            out.split_w(dve)
            with dve.Fori(0, ROWS // 2) as i:
                columns(i, lambda row, xx: out.split_lo(dve, row, xx),
                        lambda row, k, xx: out.evacuate(dve, row, i, k, xx, 1))


def program(nc, x, w_in_t, b_in_r, filt_t, wdw_t, b_dw_r, w_out_t, b_out_c, circ_c, shift_c, y):
    B, D, H, W = x.shape
    C = w_in_t.shape[1]
    PAIRS, BY, BX = B // IMG, H // BLK_Y, W // BLK_X
    assert PAIRS == 4 and C // GRP == 2 * 2 * BY
    e_dram = nc.dram_tensor("composites", [C // GRP, 128, GRP, REACH], F32).ap()
    h_dram = [nc.dram_tensor(f"hidden{q}", [C // GRP, 128, BY, 2, GRP, BX // 2 * IMG], F32).ap() for q in range(PAIRS)]
    g_dram = [nc.dram_tensor(f"gelu{q}", [C, 128, (BY + 1) * (BX + 1) * IMG], F32).ap() for q in range(PAIRS)]
    build_composites(nc, filt_t, wdw_t, circ_c, shift_c, e_dram)
    conv_in_alone(nc, x, w_in_t, 0, h_dram[0:2])
    spatial_beside_conv_in(nc, b_in_r, b_dw_r, e_dram, h_dram[0:2], g_dram[0:2], x, w_in_t, 2, h_dram[2:4])
    spatial_beside_conv_out(nc, b_in_r, b_dw_r, e_dram, h_dram[2:4], g_dram[2:4], w_out_t, b_out_c, 0, g_dram[0:2], y)
    conv_out_alone(nc, w_out_t, b_out_c, 2, g_dram[2:4], y)


def shape_constants():
    ky, kx, xi, u, x = np.ogrid[0:PATCH, 0:PATCH // 2 + 1, 0:PATCH, 0:2 * PATCH, 0:PATCH]
    twice = np.where((kx == 0) | (kx == PATCH // 2), 1.0, 2.0)
    circ = twice * np.cos(2 * np.pi * ((ky * u + kx * (x - xi)) % PATCH) / PATCH) / (PATCH * PATCH)
    i, j, X, u, x = np.ogrid[0:TAPS, 0:TAPS, 0:SPREAD, 0:3 * TAPS, 0:PATCH]
    shift = (u == TAPS + i) & (x == X - (TAPS - 1) + j)
    return (circ.reshape((-1,) + circ.shape[2:]).astype(np.float32),
            shift.reshape((-1,) + shift.shape[2:]).astype(np.float32))


def kernel(x, L0_conv_w_in, L0_conv_b_in, L0_conv_fft_filter, L0_conv_w_dw, L0_conv_b_dw, L0_conv_w_out,
           L0_conv_b_out):
    import concourse.bacc as bacc
    from concourse.bass_utils import run_bass_kernel_spmd

    x = np.ascontiguousarray(x)
    C = L0_conv_w_in.shape[0]
    circ, shift = shape_constants()
    rows = np.ascontiguousarray
    arrays = {
        "x": x,
        "w_in_t": rows(np.asarray(L0_conv_w_in).reshape(C, -1).T),
        "b_in_r": rows(np.asarray(L0_conv_b_in).reshape(1, C)),
        "filt_t": rows(np.asarray(L0_conv_fft_filter).reshape(C, -1).T),
        "wdw_t": rows(np.asarray(L0_conv_w_dw).reshape(C, -1).T),
        "b_dw_r": rows(np.asarray(L0_conv_b_dw).reshape(1, C)),
        "w_out_t": rows(np.asarray(L0_conv_w_out).reshape(-1, C).T),
        "b_out_c": rows(np.asarray(L0_conv_b_out).reshape(-1, 1)),
        "circ_c": circ,
        "shift_c": shift,
    }
    nc = bacc.Bacc("TRN2", target_bir_lowering=False, num_devices=1)
    args = [nc.dram_tensor(name, a.shape, mybir.dt.from_np(a.dtype), kind="ExternalInput").ap()
            for name, a in arrays.items()]
    y = nc.dram_tensor("y", x.shape, F32, kind="ExternalOutput").ap()
    program(nc, *args, y)
    return run_bass_kernel_spmd(nc, [arrays], core_ids=[0]).results[0]["y"]
```

```python
from contextlib import ExitStack

import numpy as np

import concourse.bass as bass
from concourse import mybir
from concourse.alu_op_type import AluOpType as ALU

F32 = mybir.dt.float32
F32R = mybir.dt.float32r
ACT = mybir.ActivationFunctionType

PATCH = 8
TAPS = 7
HALO = TAPS // 2
SPREAD = PATCH + 2 * HALO
BLK_Y, BLK_X = 2 * PATCH, PATCH
PX = BLK_Y * BLK_X
REACH_Y, REACH_X = 2 * BLK_Y, 2 * BLK_X
ROWS_R = PATCH + SPREAD
GRP = 4
IMG = 2
BANK = 512
START = 64


def real(ap):
    return ap.bitcast(F32R)


class Named:

    def __init__(self, nc, ctx, stage):
        self.nc, self.ctx, self.stage = nc, ctx, stage

    def sbuf(self, name, shape):
        return self.ctx.enter_context(self.nc.sbuf_tensor(f"{self.stage}_{name}", shape, F32))

    def psum(self, name, shape):
        return self.ctx.enter_context(self.nc.psum_tensor(f"{self.stage}_{name}", shape, F32))

    def sem(self, name):
        sem = self.ctx.enter_context(self.nc.semaphore(f"{self.stage}_{name}"))
        self.nc.gpsimd.sem_inc(sem, START)
        return sem


class ConvIn:

    def __init__(self, n, x, w_in_t, pair0, h_dram, banks, evacuators, slots):
        self.x, self.w_in_t, self.pair0 = x, w_in_t, pair0
        self.h_view = [h.rearrange("g p y f j b -> y f p g (j b)") for h in h_dram]
        self.C = C = w_in_t.shape[1]
        self.D = w_in_t.shape[0]
        self.HW = x.shape[3] // 2
        self.SETS = self.HW // BLK_X
        self.banks, self.slots = banks, slots
        self.xs = n.sbuf("xs", [128, slots, BLK_Y, self.HW])
        self.xsplit = n.sbuf("xsplit", [128, slots, IMG, self.SETS, PX])
        self.hs = n.sbuf("hs", [128, slots, C, self.SETS * IMG])
        self.w = n.sbuf("w_in", [128, C])
        self.whi = n.sbuf("w_in_hi", [128, C])
        self.wlo = n.sbuf("w_in_lo", [128, C])
        self.w_loaded = n.sem("w_in_loaded")
        self.w_split = n.sem("w_in_split")
        self.x_loaded = [n.sem(f"x_loaded{i}") for i in range(slots)]
        self.x_hi = n.sem("x_hi")
        self.x_lo = n.sem("x_lo")
        self.mm_done = n.sem("hidden_mm")
        self.ev = [n.sem(f"hidden_ev_{e}") for e in evacuators]
        self.stored = [n.sem(f"hidden_stored{i}") for i in range(slots)]

    def slot(self, f):
        return f % self.slots

    def before(self, ab, u):
        return ab if self.slots == 2 else u

    def load_w(self, sp):
        for half in range(2):
            sp.dma_start(self.w[64 * half:64 * half + self.D, :], self.w_in_t).then_inc(self.w_loaded, 16)

    def split_w(self, dve):
        dve.wait_ge(self.w_loaded, START + 32)
        dve.tensor_copy(real(self.whi[:, :]), self.w[:, :]).then_inc(self.w_split, 1)
        dve.wait_ge(self.w_split, START + 1)
        dve.tensor_tensor(real(self.wlo[:, :]), self.w[:, :], self.whi[:, :], ALU.subtract).then_inc(self.w_split, 1)

    def load(self, sp, a, b, f, u):
        sp.wait_ge(self.x_hi, u * IMG + (START - IMG * (self.slots - 1)))
        sp.wait_ge(self.x_lo, u * IMG + (START - IMG * (self.slots - 1)))
        q = (self.pair0 + a) * IMG
        src = self.x[q:q + IMG, :, bass.ds(b * BLK_Y, BLK_Y), f * self.HW:(f + 1) * self.HW]
        sp.dma_start(self.xs[:, self.slot(f)], src.rearrange("i c r w -> (i c) r w")
                     ).then_inc(self.x_loaded[self.slot(f)], 16)

    def store(self, sp, a, b, f, u):
        for ev in self.ev:
            sp.wait_ge(ev, u * (self.SETS // len(self.ev)) + (START + self.SETS // len(self.ev)))
        half = self.C // 2
        for c0 in range(0, self.C, half):
            sp.dma_start(self.h_view[a][b, f, :, c0 // GRP:(c0 + half) // GRP, :],
                         self.hs[:, self.slot(f), c0:c0 + half, :].rearrange("p (g j) b -> p g (j b)", j=GRP)
                         ).then_inc(self.stored[self.slot(f)], 16)

    def stored_all(self, sp, units):
        for sem in self.stored:
            sp.wait_ge(sem, START + 32 * units // self.slots)

    def _images(self, eng, ab, f, u):
        k = self.slot(f)
        eng.wait_ge(self.x_loaded[k], self.before(ab, u) * 16 + (START + 16))
        eng.wait_ge(self.mm_done, u * self.SETS + (START - self.SETS * (self.slots - 1)))
        for img in range(IMG):
            own, other = slice(64 * img, 64 * img + 64), slice(64 - 64 * img, 128 - 64 * img)
            blocks = self.xsplit[:, k, img].rearrange("p b (r x) -> p r b x", x=BLK_X)
            raw = self.xs[own, k].rearrange("p r (b x) -> p r b x", x=BLK_X)
            yield img, raw, blocks[own], blocks[other]

    def split_hi(self, act, ab, f, u):
        for img, raw, hi, lo in self._images(act, ab, f, u):
            act.copy(real(hi), raw).then_inc(self.x_hi, 1)

    def split_lo(self, dve, ab, f, u):
        for img, raw, hi, lo in self._images(dve, ab, f, u):
            dve.wait_ge(self.x_hi, u * IMG + (START + 1 + img))
            dve.tensor_tensor(real(lo), raw, hi, ALU.subtract).then_inc(self.x_lo, 1)

    def products(self, pe, f, u, m):
        if m == 0:
            pe.wait_ge(self.x_lo, u * IMG + (START + IMG))
        E, NB = len(self.ev), len(self.banks)
        pe.wait_ge(self.ev[m % E], u * (self.SETS // E) + (START + (m - NB) // E + 1))
        for img in range(IMG):
            out = self.banks[m % NB][:, img * self.C:(img + 1) * self.C]
            lhs = real(self.xsplit[:, self.slot(f), img, m, :])
            pe.matmul(out, lhs, real(self.whi[:, :]), start=True, stop=False)
            mm = pe.matmul(out, lhs, real(self.wlo[:, :]), start=False, stop=True)
        mm.then_inc(self.mm_done, 1)

    def evacuate(self, eng, copy, ab, f, u, m):
        if m < len(self.ev):
            eng.wait_ge(self.stored[self.slot(f)], self.before(ab, u) * 32 + START)
        eng.wait_ge(self.mm_done, u * self.SETS + (START + m + 1))
        copy(self.hs[:, self.slot(f), :, IMG * m:IMG * (m + 1)],
             self.banks[m % len(self.banks)].rearrange("p (i c) -> p c i", i=IMG)
             ).then_inc(self.ev[m % len(self.ev)], 1)


class Spatial:

    def __init__(self, n, b_in_r, b_dw_r, e_dram, h_dram, g_dram, by_act):
        self.by_act = by_act
        self.PAIRS = len(h_dram)
        self.GROUPS, _, self.BY, _, _, self.HALF = h_dram[0].shape
        self.C = C = self.GROUPS * GRP
        self.ROW = 2 * self.HALF
        self.TY, self.TROW = self.BY + 1, self.ROW + IMG
        self.CUTS = [0, 6, 12, self.TY]
        self.BANKS = len(self.CUTS) - 1
        self.b_in_r, self.b_dw_r, self.e_dram, self.h_dram, self.g_dram = b_in_r, b_dw_r, e_dram, h_dram, g_dram
        assert self.PAIRS == 2
        self.b_in = n.sbuf("b_in", [128, C])
        self.b_dw = n.sbuf("b_dw", [128, C])
        self.bias = n.sbuf("bias", [128, GRP])
        self.eraw = n.sbuf("eraw", [128, GRP, ROWS_R, 2, BLK_X])
        self.ehi = n.sbuf("ehi", [128, GRP, 2, REACH_Y, BLK_X])
        self.elo = n.sbuf("elo", [128, GRP, 2, REACH_Y, BLK_X])
        self.h = n.sbuf("h", [128, self.PAIRS, self.BY, 2, GRP, self.HALF])
        self.hi = n.sbuf("hi", [128, GRP, self.BY, 2, self.HALF])
        self.low = n.sbuf("low", [128, GRP, self.BY, 2, self.HALF])
        self.g = n.sbuf("g", [128, GRP, self.TY * self.TROW])
        self.ps = [n.psum(f"ps{i}", [128, self.BANKS, BANK]) for i in range(2)]
        self.b_loaded = n.sem("b_loaded")
        self.bias_here = n.sem("bias_here")
        self.e_loaded = n.sem("e_loaded")
        self.h_loaded = [n.sem(f"h_loaded{i}") for i in range(self.PAIRS)]
        self.e_zero = n.sem("e_zero")
        self.e_hi = n.sem("e_hi")
        self.e_lo = n.sem("e_lo")
        self.h_hi = n.sem("h_hi")
        self.h_lo = n.sem("h_lo")
        self.low_dve = n.sem("low_dve")
        self.low_act = n.sem("low_act")
        self.mm_done = n.sem("mm_done")
        self.g_done = n.sem("g_done")
        self.stored = [n.sem(f"g_stored{i}") for i in range(GRP)]
        self.PER = self.PAIRS * GRP


    def load_biases(self, sp):
        for t, src in ((self.b_in, self.b_in_r), (self.b_dw, self.b_dw_r)):
            sp.dma_start(t[:], src.to_broadcast([128, self.C])).then_inc(self.b_loaded, 16)

    def load_e(self, sp, c):
        sp.wait_ge(self.e_lo, c * GRP + START)
        sp.dma_start(self.eraw[:].rearrange("p c r d x -> p c (r d x)"), self.e_dram[c]).then_inc(self.e_loaded, 16)

    def load_h(self, sp, c, q):
        sp.wait_ge(self.mm_done, c * (self.PER * self.BANKS) + (START + (q * GRP + GRP - self.PER) * self.BANKS))
        sp.dma_start(self.h[:, q].rearrange("p y f j b -> p (y f j b)"),
                     self.h_dram[q][c].rearrange("p y f j b -> p (y f j b)")).then_inc(self.h_loaded[q], 16)

    def store(self, sp, c, q, j):
        sp.wait_ge(self.g_done, c * (self.PER * self.BANKS) + (START + (q * GRP + j + 1) * self.BANKS))
        late = HALO * BLK_X
        for px, t0 in ((slice(0, late), self.TROW), (slice(late, PX), 0)):
            sp.dma_start(self.g_dram[q][bass.ds(c * GRP + j, 1), px, :].rearrange("j p t -> (j p) t"),
                         self.g[px, j, t0:t0 + self.BY * self.TROW]).then_inc(self.stored[j], 16)

    def stored_all(self, sp):
        for sem in self.stored:
            sp.wait_ge(sem, START + 32 * self.PAIRS * self.GROUPS)

    def clear_e(self, dve):
        for e in (self.ehi, self.elo):
            dve.memset(e[:, :, :, ROWS_R:REACH_Y].rearrange("p j d r x -> p (j d) (r x)"), 0.0).then_inc(self.e_zero, 1)
        dve.wait_ge(self.e_zero, START + 2)

    def split(self, dve, c, q, j):
        w = q * GRP + j
        if w == 0:
            dve.wait_ge(self.b_loaded, START + 32)
        if j == 0:
            dve.wait_ge(self.h_loaded[q], c * 16 + (START + 16))
        raw = self.h[:, q, :, :, j, :].rearrange("p y f b -> p (y f) b")
        big = self.hi[:, j].rearrange("p y f b -> p (y f) b")
        low = self.low[:, j].rearrange("p y f b -> p (y f) b")
        bias = self.b_in[:, bass.ds(c * GRP + j, 1)]
        dve.wait_ge(self.mm_done, c * (self.PER * self.BANKS) + (START + (w - GRP + 1) * self.BANKS))
        dve.tensor_scalar(real(big), raw, bias, None, ALU.add).then_inc(self.h_hi, 1)
        dve.wait_ge(self.h_hi, c * self.PER + (START + w + 1))
        dve.scalar_tensor_tensor(real(raw), raw, bias, big, ALU.add, ALU.subtract).then_inc(self.h_lo, 1)
        if w not in self.by_act:
            dve.tensor_copy(real(low[64:128]), big[64:128]).then_inc(self.low_dve, 1)
        dve.wait_ge(self.h_lo, c * self.PER + (START + w + 1))
        dve.tensor_copy(real(low[0:64]), raw[64:128]).then_inc(self.low_dve, 1)
        if q == 0:
            if j == 0:
                dve.wait_ge(self.e_loaded, c * 16 + (START + 16))
            eraw = self.eraw[:, j].rearrange("p r d x -> p d r x")
            dve.tensor_copy(real(self.ehi[:, j, :, 0:ROWS_R]), eraw).then_inc(self.e_hi, 1)
            dve.wait_ge(self.e_hi, c * GRP + (START + j + 1))
            dve.tensor_tensor(real(self.elo[:, j, :, 0:ROWS_R]), eraw, self.ehi[:, j, :, 0:ROWS_R], ALU.subtract
                              ).then_inc(self.e_lo, 1)

    def low_from_hi(self, act, c, q, j):
        w = q * GRP + j
        act.wait_ge(self.h_hi, c * self.PER + (START + w + 1))
        act.copy(real(self.low[64:128, j]), self.hi[64:128, j]).then_inc(self.low_act, 1)

    def products(self, pe, c, q, j, between):
        w = q * GRP + j
        theirs = sum(v in self.by_act for v in range(w + 1))
        pe.wait_ge(self.low_dve, c * (2 * self.PER - len(self.by_act)) + (START + 2 * (w + 1) - theirs))
        if q == 0:
            pe.wait_ge(self.e_lo, c * GRP + (START + j + 1))
        for b in range(self.BANKS):
            pe.wait_ge(self.g_done, c * (self.PER * self.BANKS) + (START + (w - 2) * self.BANKS + b + 1))
            t0, t1 = self.CUTS[b], self.CUTS[b + 1]
            lo = self.h[:, q, :, :, j, :]
            parts = [(0, dx, e, v) for dx in range(2)
                     for e, v in ((self.ehi, self.hi[:, j]), (self.ehi, lo), (self.elo, self.hi[:, j]))]
            parts += [(1, dx, e, self.low[:, j]) for dx in range(2) for e in (self.ehi, self.elo)]
            for m, (dy, dx, e, v) in enumerate(parts):
                r0, r1 = max(t0 - dy, 0), min(t1 - dy, self.BY)
                out = self.ps[j % 2][:, b, 0:(t1 - t0) * self.TROW].rearrange("p (t c) -> p t c", c=self.TROW)
                out = out[:, r0 + dy - t0:r1 + dy - t0, IMG * dx:IMG * dx + self.ROW]
                if b == 0 and m == len(parts) - 4 and w in self.by_act:
                    pe.wait_ge(self.low_act, c * len(self.by_act) + (START + theirs))
                mm = pe.matmul(out.rearrange("p t (f b) -> p t f b", f=2),
                               real(e[:, j, dx, BLK_Y * dy:BLK_Y * (dy + 1), :].rearrange("p y x -> p (y x)")),
                               real(v[:, r0:r1]), start=m == 0, stop=m == len(parts) - 1, skip_group_check=True)
            mm.then_inc(self.mm_done, 1)
            between(b)

    def biases(self, act, c):
        act.wait_ge(self.g_done, c * (self.PER * self.BANKS) + START)
        act.wait_ge(self.b_loaded, START + 32)
        act.copy(self.bias[:, :], self.b_dw[:, bass.ds(c * GRP, GRP)]).then_inc(self.bias_here, 1)
        act.wait_ge(self.bias_here, c + (START + 1))

    def gelu(self, act, c, q, j, b):
        w = q * GRP + j
        if b == 0:
            act.wait_ge(self.stored[j], c * (32 * self.PAIRS) + (START + 32 * q))
        act.wait_ge(self.mm_done, c * (self.PER * self.BANKS) + (START + w * self.BANKS + b + 1))
        t0, t1 = self.CUTS[b] * self.TROW, self.CUTS[b + 1] * self.TROW
        act.activation(self.g[:, j, t0:t1], self.ps[j % 2][:, b, 0:t1 - t0], ACT.Gelu, bias=self.bias[:, j:j + 1]
                       ).then_inc(self.g_done, 1)


class ConvOut:

    def __init__(self, n, w_out_t, b_out_c, pair0, g_dram, y, banks, slots):
        self.w_out_t, self.b_out_c, self.pair0, self.g_dram, self.y = w_out_t, b_out_c, pair0, g_dram, y
        self.C, self.D = w_out_t.shape
        self.KH = KH = self.C // 128
        H, W = y.shape[2:]
        self.TY, self.TX = H // BLK_Y, W // BLK_X
        self.TROW, self.ROWN = (self.TX + 1) * IMG, self.TX * IMG
        self.banks, self.slots = banks, slots
        self.w = n.sbuf("w_out", [128, KH, self.D])
        self.parts = n.sbuf("w_out_parts", [128, KH, 2, self.D])
        self.bias = n.sbuf("b_out", [self.D, 1])
        self.aside = n.sbuf("aside", [self.D, len(banks), BANK])
        self.graw = n.sbuf("graw", [128, slots, KH, self.TY * self.TROW])
        self.ghi = n.sbuf("ghi", [128, 2, KH, self.TY, self.ROWN])
        self.yb = n.sbuf("yb", [2 * self.D, IMG, self.TY, W])
        self.w_loaded = n.sem("w_out_loaded")
        self.w_split = n.sem("w_out_split")
        self.g_loaded = [n.sem(f"g_loaded{i}") for i in range(slots)]
        self.g_hi = n.sem("g_hi")
        self.g_lo = n.sem("g_lo")
        self.mm_done = n.sem("y_mm")
        self.set_aside = n.sem("y_aside")
        self.added = n.sem("y_added")
        self.stored = [n.sem(f"y_stored{i}") for i in range(2)]

    def load_w(self, sp):
        sp.dma_start(self.w[:], self.w_out_t.rearrange("(f p) d -> p f d", p=128)).then_inc(self.w_loaded, 16)
        sp.dma_start(self.bias[:], self.b_out_c).then_inc(self.w_loaded, 16)

    def split_w(self, dve):
        dve.wait_ge(self.w_loaded, START + 32)
        hi, lo = self.parts[:, :, 0, :], self.parts[:, :, 1, :]
        dve.tensor_copy(real(hi), self.w[:]).then_inc(self.w_split, 1)
        dve.wait_ge(self.w_split, START + 1)
        dve.tensor_tensor(real(lo), self.w[:], hi, ALU.subtract).then_inc(self.w_split, 1)

    def load(self, sp, a, r, late, xx):
        k = xx % self.slots
        sp.wait_ge(self.mm_done, (r + a * BLK_Y) * (2 * BLK_X) + (START + 2 * (xx + 1 - self.slots)))
        px = (r + (HALO - BLK_Y if late else HALO)) * BLK_X + xx
        for f in range(self.KH):
            sp.dma_start(self.graw[:, k, f], self.g_dram[a][f * 128:(f + 1) * 128, bass.ds(px, 1), :]
                         .rearrange("c x t -> c (x t)")).then_inc(self.g_loaded[k], 16)

    def store(self, sp, a, r, k):
        sp.wait_ge(self.added, (r + a * BLK_Y) * (2 * BLK_X) + (START + 2 * BLK_X))
        for img in range(IMG):
            dst = self.y[(self.pair0 + a) * IMG + img].rearrange("d (t s) w -> d t s w", s=BLK_Y)
            sp.dma_start(dst[:, :, bass.ds(r, 1), :].rearrange("d t s w -> d t (s w)"), self.yb[k * self.D:(k + 1) * self.D, img]
                         ).then_inc(self.stored[k], 16)

    def stored_all(self, sp, rows):
        for sem in self.stored:
            sp.wait_ge(sem, START + 16 * IMG * rows // 2)

    def _window(self, k, xx):
        c0 = IMG if xx < HALO else 0
        return self.graw[:, k].rearrange("p f (t c) -> p f t c", c=self.TROW)[:, :, :, c0:c0 + self.ROWN]

    def split_hi(self, act, row, xx):
        k = xx % self.slots
        act.wait_ge(self.g_loaded[k], row * (BLK_X // self.slots * 16 * self.KH) + (START + (xx // self.slots + 1) * 16 * self.KH))
        act.wait_ge(self.mm_done, row * (2 * BLK_X) + (START + 2 * (xx - 1)))
        act.copy(real(self.ghi[:, xx % 2]), self._window(k, xx)).then_inc(self.g_hi, 1)

    def split_lo(self, dve, row, xx):
        v = self._window(xx % self.slots, xx)
        dve.wait_ge(self.g_hi, row * BLK_X + (START + xx + 1))
        dve.tensor_tensor(real(v), v, self.ghi[:, xx % 2], ALU.subtract).then_inc(self.g_lo, 1)

    def products(self, pe, row, xx, half):
        NB = len(self.banks)
        m = 2 * xx + half
        if half == 0:
            pe.wait_ge(self.g_lo, row * BLK_X + (START + xx + 1))
        pe.wait_ge(self.added, row * (2 * BLK_X) + (START + m - NB + 1))
        t0, t1 = half * self.TY // 2, (half + 1) * self.TY // 2
        lo = self._window(xx % self.slots, xx)
        hi = self.ghi[:, xx % 2]
        parts = [(f, v) for f in range(self.KH) for v in (hi, lo)]
        for i, (f, v) in enumerate(parts):
            mm = pe.matmul(self.banks[m % NB].rearrange("p (t c) -> p t c", c=self.ROWN),
                           real(self.parts[:, f].rearrange("p a d -> p (a d)")), real(v[:, f, t0:t1, :]),
                           start=i == 0, stop=i == len(parts) - 1)
        mm.then_inc(self.mm_done, 1)

    def put_aside(self, act, row, xx, half):
        m, NB = 2 * xx + half, len(self.banks)
        act.wait_ge(self.mm_done, row * (2 * BLK_X) + (START + m + 1))
        act.activation(self.aside[:, m % NB], self.banks[m % NB][self.D:2 * self.D, :], ACT.Identity,
                       bias=self.bias[:, 0:1]).then_inc(self.set_aside, 1)

    def add(self, dve, row, i, k, xx, half):
        m, NB = 2 * xx + half, len(self.banks)
        if m == 0:
            dve.wait_ge(self.stored[k], i * (16 * IMG) + START)
        dve.wait_ge(self.set_aside, row * (2 * BLK_X) + (START + m + 1))
        x = (xx - HALO) % BLK_X
        out = self.yb[k * self.D:(k + 1) * self.D].rearrange("p i t (c x) -> p i t c x", x=BLK_X)
        out = out[:, :, half * (self.TY // 2):(half + 1) * (self.TY // 2), :, x].rearrange("p i t c -> p (t c) i")
        dve.tensor_tensor(out, self.banks[m % NB][0:self.D, :].rearrange("p (c i) -> p c i", i=IMG),
                          self.aside[:, m % NB].rearrange("p (c i) -> p c i", i=IMG), ALU.add
                          ).then_inc(self.added, 1)


def composites_beside_conv_in(nc, filt_t, wdw_t, circ_c, shift_c, e_dram, x, w_in_t, h_dram):
    freqs, C = filt_t.shape
    taps = wdw_t.shape[0]
    PP, SS = PATCH * PATCH, SPREAD * SPREAD
    PARTS = 4
    CC, CS = C // PARTS, C // PARTS // 2
    SET = 2 * BANK
    K_MM, D_MM = SET // CC, SET // CS
    K_SETS, D_SETS = PP // K_MM, -(-SS // D_MM)
    SETS = K_SETS + 2 * D_SETS
    GROUPS = CS // GRP
    assert SETS % 2 == 0 and PP % K_MM == 0
    with ExitStack() as ctx:
        n = Named(nc, ctx, "comp")
        filt = n.sbuf("filt", [freqs, C])
        wdw = n.sbuf("wdw", [taps, C])
        filt_d = n.sbuf("filt_d", [128, CC])
        wdw_d = n.sbuf("wdw_d", [128, 2, CS])
        circ_hi = n.sbuf("circ_hi", [128, PATCH, 2 * PATCH, PATCH])
        circ_lo = n.sbuf("circ_lo", [128, PATCH, 2 * PATCH, PATCH])
        shift_tab = n.sbuf("shift_tab", [128, SPREAD, 3 * TAPS, PATCH])
        circ = n.sbuf("circ", [PP, PP, CC])
        shifted = n.sbuf("shifted", [PP, SS, CS])
        lhs = n.sbuf("lhs", [PP, 2, GRP, 2, PP])
        stage = n.sbuf("stage", [128, 2, GRP, ROWS_R, REACH_X])
        tp = [n.psum(f"tp{i}", [128, 2, BANK]) for i in range(2)]
        psx = n.psum("psx", [128, 4, BANK])
        loaded = n.sem("loaded")
        zeroed = n.sem("zeroed")
        tab_split = n.sem("tab_split")
        placed = n.sem("placed")
        tab_done = n.sem("tab_done")
        ev = [n.sem("ev_dve"), n.sem("ev_act")]
        lhs_ready = n.sem("lhs_ready")
        comp_done = n.sem("comp_done")
        top_done = n.sem("top_done")
        bot_done = n.sem("bot_done")
        stored = [n.sem(f"stored{i}") for i in range(2)]
        cin = ConvIn(n, x, w_in_t, 0, h_dram, [psx[:, i] for i in range(4)], ["act", "dve"], 2)
        raw = cin.hs[:, 0].rearrange("p c b -> p (c b)")
        CIRC, SHIFT = PATCH * 2 * PATCH * PATCH, SPREAD * 3 * TAPS * PATCH
        circ_raw, shift_raw = raw[:, 0:CIRC], raw[:, CIRC:CIRC + SHIFT]
        block = ctx.enter_context(nc.Block())

        def first(d, e):
            return d * (2 * GROUPS) + e * GROUPS

        @block.sync
        def _(sp):
            sp.dma_start(filt[:], filt_t).then_inc(loaded, 16)
            sp.dma_start(wdw[:], wdw_t).then_inc(loaded, 16)
            sp.dma_start(circ_raw, circ_c.rearrange("p x u v -> p (x u v)")).then_inc(loaded, 16)
            sp.dma_start(shift_raw, shift_c.rearrange("p x u v -> p (x u v)")).then_inc(loaded, 16)
            cin.load_w(sp)
            for f in range(2):
                cin.load(sp, 0, 0, f, f)
            for d in range(PARTS):
                for e in range(2):
                    a, b0 = d // 2, (d % 2 * 2 + e) * (GROUPS // 2)

                    def strip(i, last):
                        for f in range(2):
                            u = i * 2 + (first(d, e) + f)
                            if not last:
                                cin.load(sp, a, i + (b0 + 1), f, u + 2)
                            elif a == 0:
                                cin.load(sp, 1, 0, f, u + 2)
                            sp.wait_ge(top_done, u * 2 + (START + 2))
                            sp.wait_ge(bot_done, u * 2 + (START + 2))
                            sp.dma_start(e_dram[u], stage[:, f].rearrange("p c r x -> p c (r x)")
                                         ).then_inc(stored[f], 16)
                            cin.store(sp, a, i + b0, f, u)
                    if d % 2 and e:
                        with sp.Fori(0, GROUPS // 2 - 1) as i:
                            strip(i, False)
                        strip(GROUPS // 2 - 1, True)
                    else:
                        with sp.Fori(0, GROUPS // 2) as i:
                            strip(i, False)
            for k in range(2):
                sp.wait_ge(stored[k], START + 16 * PARTS * GROUPS)
            cin.stored_all(sp, 2 * PARTS * GROUPS)

        @block.tensor
        def _(pe):
            def free(d, t):
                pe.wait_ge(ev[t % 2], d * (SETS // 2) + (START + t // 2))

            pe.wait_ge(tab_split, START + 3)
            pe.wait_ge(cin.w_split, START + 2)
            with pe.Fori(0, PARTS) as d:
                pe.wait_ge(placed, d * 4 + (START + 4))
                for e in range(2):
                    pe.wait_ge(top_done, first(d, e) * 2 + START)
                    pe.wait_ge(bot_done, first(d, e) * 2 + START)
                    if e == 0:
                        for t in range(K_SETS):
                            free(d, t)
                            for m in range(K_MM):
                                yi, xi = divmod(t * K_MM + m, PATCH)
                                at = m * CC
                                for tab in (circ_hi, circ_lo):
                                    mm = pe.matmul(tp[t % 2][0:PP, at // BANK, at % BANK:at % BANK + CC],
                                                   real(tab[:, xi, PATCH - yi:2 * PATCH - yi, :]
                                                        .rearrange("p u v -> p (u v)")),
                                                   real(filt_d[:, :]), start=tab is circ_hi, stop=tab is circ_lo)
                            mm.then_inc(tab_done, 1)
                    for g in range(D_SETS):
                        t = K_SETS + e * D_SETS + g
                        free(d, t)
                        for m in range(min(D_MM, SS - g * D_MM)):
                            Y, X = divmod(g * D_MM + m, SPREAD)
                            at = m * CS
                            mm = pe.matmul(tp[t % 2][0:PP, at // BANK, at % BANK:at % BANK + CS],
                                           real(shift_tab[:, X, SPREAD - 1 - Y:SPREAD - 1 - Y + PATCH, :]
                                                .rearrange("p u v -> p (u v)")),
                                           real(wdw_d[:, e, :]), start=True, stop=True)
                        mm.then_inc(tab_done, 1)
                    upto = K_SETS + (e + 1) * D_SETS
                    with pe.Fori(0, GROUPS // 2) as i:
                        for k in range(2):
                            u = first(d, e) + (i * 2 + k)
                            pe.wait_ge(lhs_ready, u * 2 + (START + 2))
                            if k == 0:
                                pe.wait_ge(ev[0], d * (SETS // 2) + (START + (upto + 1) // 2))
                                pe.wait_ge(ev[1], d * (SETS // 2) + (START + upto // 2))
                            pe.wait_ge(top_done, u * 2 + (START - 2))
                            pe.wait_ge(bot_done, u * 2 + (START - 2))
                            for j in range(GRP):
                                mm = pe.matmul(tp[k][:, j // 2, (j % 2) * SS:(j % 2 + 1) * SS],
                                               lhs[:, k, j].rearrange("p h a -> p (h a)"),
                                               shifted[:, :, bass.ds(i * (2 * GRP) + (k * GRP + j), 1)]
                                               .rearrange("p a c -> p (a c)"),
                                               start=True, stop=True)
                            mm.then_inc(comp_done, 1)
                            for m in range(cin.SETS):
                                cin.products(pe, k, u, m)

        def evacuate(eng, d, t, copy):
            e = 0 if t < K_SETS + D_SETS else 1
            if t < K_SETS:
                eng.wait_ge(lhs_ready, first(d, 0) * 2 + START)
                out, cols = circ[:, t * K_MM:(t + 1) * K_MM, :], SET
            else:
                eng.wait_ge(comp_done, first(d, e) + START)
                g = (t - K_SETS) % D_SETS
                cnt = min(D_MM, SS - g * D_MM)
                out, cols = shifted[:, g * D_MM:g * D_MM + cnt, :], cnt * CS
            eng.wait_ge(tab_done, d * SETS + (START + t + 1))
            copy(out.rearrange("p a c -> p (a c)"),
                 tp[t % 2][0:PP, :, :].rearrange("p a c -> p (a c)")[:, 0:cols]).then_inc(ev[t % 2], 1)

        def to_stage(eng, u, ab, k, half, done, copy):
            rows = slice(PP * half, PP * (half + 1))
            r0 = PATCH * half
            eng.wait_ge(comp_done, u + (START + 1))
            eng.wait_ge(stored[k], ab * 16 + START)
            for b in range(GRP // 2):
                src = tp[k][rows, b, 0:2 * SS].rearrange("p (c r x) -> p c r x", c=2, x=SPREAD)
                if half == 0:
                    copy(stage[rows, k, 2 * b:2 * b + 2, BLK_Y:ROWS_R, 0:SPREAD], src[:, :, PATCH:SPREAD, :])
                copy(stage[rows, k, 2 * b:2 * b + 2, r0:r0 + SPREAD, 0:SPREAD], src).then_inc(done, 1)

        def quarters(eng, parity, half, done, copy, quarter_start, split, pick):
            def group(d, e, i, k, last):
                ab = d * GROUPS + e * (GROUPS // 2) + i
                u = ab * 2 + k
                pick(i, k, e, u)
                if not last:
                    split(eng, ab + k, 1 - k, u + 1)
                to_stage(eng, u, ab, k, half, done, copy)
                for m in range(1 - parity, cin.SETS, 2):
                    cin.evacuate(eng, copy, ab, k, u, m)

            def quarter(d, last):
                quarter_start(d)
                for e in range(2):
                    for t in range(0 if e == 0 else K_SETS + D_SETS, K_SETS + (e + 1) * D_SETS):
                        if t % 2 == parity:
                            evacuate(eng, d, t, copy)
                    cut = 1 if last and e else 0
                    with eng.Fori(0, GROUPS // 2 - cut) as i:
                        for k in range(2):
                            group(d, e, i, k, False)
                    if cut:
                        for k in range(2):
                            group(d, e, GROUPS // 2 - 1, k, k == 1)

            split(eng, 0, 0, 0)
            with eng.Fori(0, PARTS - 1) as d:
                quarter(d, False)
            quarter(PARTS - 1, True)

        @block.scalar
        def _(act):
            act.wait_ge(zeroed, START + 1)
            quarters(act, 1, 0, top_done, act.copy, lambda d: None, cin.split_hi, lambda i, k, e, u: None)

        @block.vector
        def _(dve):
            def place(d):
                parts = ((filt_d[:, :], filt, freqs), (wdw_d[:].rearrange("p e c -> p (e c)"), wdw, taps))
                dve.wait_ge(tab_done, d * SETS + START)
                dve.wait_ge(loaded, START + 64)
                for to, raw, rows in parts:
                    dve.tensor_copy(real(to[0:rows]), raw[:, bass.ds(d * CC, CC)]).then_inc(placed, 1)
                dve.wait_ge(placed, d * 4 + (START + 2))
                for to, raw, rows in parts:
                    dve.tensor_tensor(real(to[64:64 + rows]), raw[:, bass.ds(d * CC, CC)], to[0:rows], ALU.subtract
                                      ).then_inc(placed, 1)

            def pick(i, k, e, u):
                dve.wait_ge(comp_done, u + (START - 1))
                for half in range(2):
                    dve.tensor_copy(lhs[:, k, :, half, :],
                                    circ[:, :, bass.ds(i * (2 * GRP) + (e * CS + k * GRP), GRP)]
                                    .rearrange("p a c -> p c a")).then_inc(lhs_ready, 1)

            dve.memset(stage[:], 0.0).then_inc(zeroed, 1)
            dve.memset(filt_d[:], 0.0).then_inc(zeroed, 1)
            dve.memset(wdw_d[:], 0.0).then_inc(zeroed, 1)
            dve.wait_ge(zeroed, START + 3)
            dve.wait_ge(loaded, START + 64)
            dve.tensor_copy(real(shift_tab[:].rearrange("p x u v -> p (x u v)")), shift_raw).then_inc(tab_split, 1)
            hi, lo = (t[:].rearrange("p x u v -> p (x u v)") for t in (circ_hi, circ_lo))
            dve.tensor_copy(real(hi), circ_raw).then_inc(tab_split, 1)
            dve.wait_ge(tab_split, START + 2)
            dve.tensor_tensor(real(lo), circ_raw, hi, ALU.subtract).then_inc(tab_split, 1)
            cin.split_w(dve)
            quarters(dve, 0, 1, bot_done, dve.tensor_copy, place, cin.split_lo, pick)


def spatial_beside_conv_in(nc, b_in_r, b_dw_r, e_dram, h_dram, g_dram, x, w_in_t, pair0, h_next):
    with ExitStack() as ctx:
        n = Named(nc, ctx, "sci")
        sp_ = Spatial(n, b_in_r, b_dw_r, e_dram, h_dram, g_dram, ())
        ps = n.psum("psx", [128, 2, BANK])
        cin = ConvIn(n, x, w_in_t, pair0, h_next, [ps[:, i] for i in range(2)], ["act"], 1)
        block = ctx.enter_context(nc.Block())
        STRIPS = x.shape[2] // BLK_Y
        places = [(w, b) for w in range(2, 8) for b in range(3)][:cin.SETS]

        @block.sync
        def _(sp):
            sp_.load_h(sp, 0, 0)
            sp_.load_biases(sp)
            cin.load_w(sp)
            sp_.load_e(sp, 0)
            cin.load(sp, 0, 0, 0, 0)
            for a in range(2):
                def group(b, k, last):
                    c = b * 2 + (a * 2 * STRIPS + k)
                    sp_.load_h(sp, c, 1)
                    if not (last and a == 1):
                        if k == 0:
                            cin.load(sp, a, b, 1, c + 1)
                        elif not last:
                            cin.load(sp, a, b + 1, 0, c + 1)
                        else:
                            cin.load(sp, 1, 0, 0, c + 1)
                        sp_.load_e(sp, c + 1)
                        sp_.load_h(sp, c + 1, 0)
                    cin.store(sp, a, b, k, c)
                with sp.Fori(0, STRIPS - 1) as b:
                    group(b, 0, False)
                    group(b, 1, False)
                group(STRIPS - 1, 0, False)
                group(STRIPS - 1, 1, True)
            sp_.stored_all(sp)
            cin.stored_all(sp, sp_.GROUPS)

        @block.tensor
        def _(pe):
            pe.wait_ge(cin.w_split, START + 2)
            with pe.Fori(0, sp_.GROUPS // 2) as ab:
                for k in range(2):
                    c = ab * 2 + k
                    for w in range(sp_.PER):
                        def between(b):
                            if (w, b) in places:
                                cin.products(pe, k, c, places.index((w, b)))
                        sp_.products(pe, c, w // GRP, w % GRP, between)

        @block.scalar
        def _(act):
            with act.Fori(0, sp_.GROUPS // 2) as ab:
                for k in range(2):
                    c = ab * 2 + k
                    cin.split_hi(act, ab, k, c)
                    sp_.biases(act, c)
                    for w in range(sp_.PER):
                        for b in range(sp_.BANKS):
                            sp_.gelu(act, c, w // GRP, w % GRP, b)
                            if (w, b) in places:
                                cin.evacuate(act, act.copy, ab, k, c, places.index((w, b)))
                        sp_.store(act, c, w // GRP, w % GRP)

        @block.vector
        def _(dve):
            sp_.clear_e(dve)
            cin.split_w(dve)
            with dve.Fori(0, sp_.GROUPS // 2) as ab:
                for k in range(2):
                    c = ab * 2 + k
                    for w in range(sp_.PER):
                        sp_.split(dve, c, w // GRP, w % GRP)
                        if w == GRP - 1:
                            cin.split_lo(dve, ab, k, c)


def spatial_beside_conv_out(nc, b_in_r, b_dw_r, e_dram, h_dram, g_dram, w_out_t, b_out_c, pair0, g_before, y):
    with ExitStack() as ctx:
        n = Named(nc, ctx, "sco")
        sp_ = Spatial(n, b_in_r, b_dw_r, e_dram, h_dram, g_dram, (2, 4, 7))
        ps = n.psum("psy", [128, 2, BANK])
        out = ConvOut(n, w_out_t, b_out_c, pair0, g_before, y, [ps[:, i] for i in range(2)], 4)
        block = ctx.enter_context(nc.Block())
        FIRST = BLK_Y - HALO
        places = [(1, 2), (2, 2), (3, 2), (4, 2), (5, 0), (5, 2), (6, 2), (7, 2)]
        hi_at = {0: [0], 2: [1], 4: [2], 5: [3]}
        lo_at = {0: [0], 2: [1], 4: [2], 5: [3]}

        @block.sync
        def _(sp):
            sp_.load_h(sp, 0, 0)
            sp_.load_biases(sp)
            out.load_w(sp)
            sp_.load_e(sp, 0)
            for xx in range(4):
                out.load(sp, 0, 0, 0, xx)
            for a in range(2):
                def row_step(b, odd, first):
                    still = isinstance(b, int)
                    for k in range(2):
                        last = a == 1 and still and b == BLK_Y - 1 and k == 1
                        c = b * 2 + (a * 2 * BLK_Y + k)
                        sp_.load_h(sp, c, 1)
                        if k == 0 and not first:
                            out.store(sp, a, b - 1, 1 - odd)
                        elif k == 0 and a:
                            out.store(sp, 0, BLK_Y - 1, 1)
                        ahead(b, k, 0, still)
                        if not last:
                            sp_.load_e(sp, c + 1)
                            sp_.load_h(sp, c + 1, 0)
                        for m in range(1, 4):
                            ahead(b, k, m, still)

                def ahead(b, k, m, still):
                    xx = 4 * k + m + 4
                    if xx < BLK_X:
                        out.load(sp, a, b, int(still and b >= FIRST), xx)
                    elif not still or b + 1 < BLK_Y:
                        out.load(sp, a, b + 1, int(still and b + 1 >= FIRST), xx - BLK_X)
                    elif a == 0:
                        out.load(sp, 1, 0, 0, xx - BLK_X)

                row_step(0, 0, True)
                LOOPS = (FIRST - 2) // 2
                with sp.Fori(0, LOOPS) as i:
                    for odd in (1, 0):
                        row_step(i * 2 + (2 - odd), odd, False)
                for b in range(2 * LOOPS + 1, BLK_Y):
                    row_step(b, b % 2, False)
            out.store(sp, 1, BLK_Y - 1, 1)
            sp_.stored_all(sp)
            out.stored_all(sp, 2 * BLK_Y)

        @block.tensor
        def _(pe):
            pe.wait_ge(out.w_split, START + 2)
            with pe.Fori(0, sp_.GROUPS // 2) as row:
                for k in range(2):
                    c = row * 2 + k
                    for w in range(sp_.PER):
                        def between(b):
                            if (w, b) in places:
                                m = places.index((w, b))
                                out.products(pe, row, 4 * k + m // 2, m % 2)
                        sp_.products(pe, c, w // GRP, w % GRP, between)

        @block.scalar
        def _(act):
            act.wait_ge(out.w_loaded, START + 32)
            with act.Fori(0, sp_.GROUPS // 2) as row:
                for k in range(2):
                    c = row * 2 + k
                    sp_.biases(act, c)
                    for w in range(sp_.PER):
                        for m in hi_at.get(w, []):
                            out.split_hi(act, row, 4 * k + m)
                        for b in range(sp_.BANKS):
                            if b == sp_.BANKS - 1 and w + 1 in sp_.by_act:
                                sp_.low_from_hi(act, c, (w + 1) // GRP, (w + 1) % GRP)
                            sp_.gelu(act, c, w // GRP, w % GRP, b)
                            if (w, b) in places:
                                m = places.index((w, b))
                                out.put_aside(act, row, 4 * k + m // 2, m % 2)
                        sp_.store(act, c, w // GRP, w % GRP)

        @block.vector
        def _(dve):
            sp_.clear_e(dve)
            out.split_w(dve)

            def group(c, row, i, odd, k, last):
                for w in range(sp_.PER):
                    v = (w + 2) % sp_.PER
                    if v > w:
                        sp_.split(dve, c, v // GRP, v % GRP)
                    elif not last:
                        sp_.split(dve, c + 1, v // GRP, v % GRP)
                    for m in lo_at.get(w, []):
                        out.split_lo(dve, row, 4 * k + m)
                    for m, (step, b) in enumerate(places):
                        if step == w:
                            out.add(dve, row, i, odd, 4 * k + m // 2, m % 2)

            for w in range(2):
                sp_.split(dve, 0, w // GRP, w % GRP)
            PAIRS_OF_ROWS = sp_.GROUPS // 4
            with dve.Fori(0, PAIRS_OF_ROWS - 1) as i:
                for odd in range(2):
                    for k in range(2):
                        group(i * 4 + (odd * 2 + k), i * 2 + odd, i, odd, k, False)
            i = PAIRS_OF_ROWS - 1
            for odd in range(2):
                for k in range(2):
                    group(i * 4 + odd * 2 + k, i * 2 + odd, i, odd, k, odd and k)


def conv_out_alone(nc, w_out_t, b_out_c, pair0, g_dram, y):
    ROWS = 2 * BLK_Y
    with ExitStack() as ctx:
        n = Named(nc, ctx, "cout")
        ps = n.psum("ps", [128, 8, BANK])
        out = ConvOut(n, w_out_t, b_out_c, pair0, g_dram, y, [ps[:, i] for i in range(8)], 8)
        block = ctx.enter_context(nc.Block())
        FIRST = BLK_Y - HALO

        @block.sync
        def _(sp):
            out.load_w(sp)
            for xx in range(BLK_X):
                out.load(sp, 0, 0, 0, xx)
            for a in range(2):
                def row_step(r, k):
                    for xx in range(BLK_X):
                        if not isinstance(r, int) or r + 1 < BLK_Y:
                            out.load(sp, a, r + 1, int(isinstance(r, int) and r + 1 >= FIRST), xx)
                        elif a == 0:
                            out.load(sp, 1, 0, 0, xx)
                    out.store(sp, a, r, k)
                with sp.Fori(0, FIRST // 2) as i:
                    for k in range(2):
                        row_step(i * 2 + k, k)
                for r in range(FIRST // 2 * 2, BLK_Y):
                    row_step(r, r % 2)
            out.stored_all(sp, ROWS)

        @block.tensor
        def _(pe):
            pe.wait_ge(out.w_split, START + 2)
            with pe.Fori(0, ROWS) as row:
                for xx in range(BLK_X):
                    for half in range(2):
                        out.products(pe, row, xx, half)

        def columns(i, split, finish):
            order = [(k, xx) for k in range(2) for xx in range(BLK_X)]
            for m in range(len(order) + 1):
                if m < len(order):
                    k, xx = order[m]
                    split(i * 2 + k, xx)
                if m:
                    k, xx = order[m - 1]
                    for half in range(2):
                        finish(i * 2 + k, k, xx, half)

        @block.scalar
        def _(act):
            act.wait_ge(out.w_loaded, START + 32)
            with act.Fori(0, ROWS // 2) as i:
                columns(i, lambda row, xx: out.split_hi(act, row, xx),
                        lambda row, k, xx, half: out.put_aside(act, row, xx, half))

        @block.vector
        def _(dve):
            out.split_w(dve)
            with dve.Fori(0, ROWS // 2) as i:
                columns(i, lambda row, xx: out.split_lo(dve, row, xx),
                        lambda row, k, xx, half: out.add(dve, row, i, k, xx, half))


def program(nc, x, w_in_t, b_in_r, filt_t, wdw_t, b_dw_r, w_out_t, b_out_c, circ_c, shift_c, y):
    B, D, H, W = x.shape
    C = w_in_t.shape[1]
    PAIRS, BY, BX = B // IMG, H // BLK_Y, W // BLK_X
    assert PAIRS == 4 and C // GRP == 2 * 2 * BY
    e_dram = nc.dram_tensor("composites", [C // GRP, 128, GRP, ROWS_R * REACH_X], F32).ap()
    h_dram = [nc.dram_tensor(f"hidden{q}", [C // GRP, 128, BY, 2, GRP, BX // 2 * IMG], F32).ap() for q in range(PAIRS)]
    g_dram = [nc.dram_tensor(f"gelu{q}", [C, 128, BY * (BX + 1) * IMG], F32).ap() for q in range(PAIRS)]
    composites_beside_conv_in(nc, filt_t, wdw_t, circ_c, shift_c, e_dram, x, w_in_t, h_dram[0:2])
    spatial_beside_conv_in(nc, b_in_r, b_dw_r, e_dram, h_dram[0:2], g_dram[0:2], x, w_in_t, 2, h_dram[2:4])
    spatial_beside_conv_out(nc, b_in_r, b_dw_r, e_dram, h_dram[2:4], g_dram[2:4], w_out_t, b_out_c, 0, g_dram[0:2], y)
    conv_out_alone(nc, w_out_t, b_out_c, 2, g_dram[2:4], y)


def shape_constants():
    ky, kx, xi, u, x = np.ogrid[0:PATCH, 0:PATCH // 2 + 1, 0:PATCH, 0:2 * PATCH, 0:PATCH]
    twice = np.where((kx == 0) | (kx == PATCH // 2), 1.0, 2.0)
    circ = twice * np.cos(2 * np.pi * ((ky * u + kx * (x - xi)) % PATCH) / PATCH) / (PATCH * PATCH)
    i, j, X, u, x = np.ogrid[0:TAPS, 0:TAPS, 0:SPREAD, 0:3 * TAPS, 0:PATCH]
    shift = (u == TAPS + i) & (x == X - (TAPS - 1) + j)

    def twice_over(table, rows):
        out = np.zeros((2, 64) + table.shape[2:], np.float32)
        out[:, :rows] = table.reshape((rows,) + table.shape[2:])
        return out.reshape((128,) + table.shape[2:])
    return twice_over(circ, PATCH * (PATCH // 2 + 1)), twice_over(shift, TAPS * TAPS)


def kernel(x, L0_conv_w_in, L0_conv_b_in, L0_conv_fft_filter, L0_conv_w_dw, L0_conv_b_dw, L0_conv_w_out,
           L0_conv_b_out):
    import concourse.bacc as bacc
    from concourse.bass_utils import run_bass_kernel_spmd

    x = np.ascontiguousarray(x)
    C = L0_conv_w_in.shape[0]
    circ, shift = shape_constants()
    rows = np.ascontiguousarray
    arrays = {
        "x": x,
        "w_in_t": rows(np.asarray(L0_conv_w_in).reshape(C, -1).T),
        "b_in_r": rows(np.asarray(L0_conv_b_in).reshape(1, C)),
        "filt_t": rows(np.asarray(L0_conv_fft_filter).reshape(C, -1).T),
        "wdw_t": rows(np.asarray(L0_conv_w_dw).reshape(C, -1).T),
        "b_dw_r": rows(np.asarray(L0_conv_b_dw).reshape(1, C)),
        "w_out_t": rows(np.asarray(L0_conv_w_out).reshape(-1, C).T),
        "b_out_c": rows(np.asarray(L0_conv_b_out).reshape(-1, 1)),
        "circ_c": circ,
        "shift_c": shift,
    }
    nc = bacc.Bacc("TRN2", target_bir_lowering=False, num_devices=1)
    args = [nc.dram_tensor(name, a.shape, mybir.dt.from_np(a.dtype), kind="ExternalInput").ap()
            for name, a in arrays.items()]
    y = nc.dram_tensor("y", x.shape, F32, kind="ExternalOutput").ap()
    program(nc, *args, y)
    return run_bass_kernel_spmd(nc, [arrays], core_ids=[0]).results[0]["y"]
```
